# Optimizing a Trainium2 kernel written in Bass

```python
import numpy as np
import jax
import jax.numpy as jnp

def _softmax(x, axis=-1):
    return jax.nn.softmax(x, axis=axis)

def _gelu(x):
    return jax.nn.gelu(x, approximate=True)

def _silu(x):
    return jax.nn.silu(x)

def _sigmoid(x):
    return jax.nn.sigmoid(x)

def _layernorm(x, axis=-1, eps=1e-05):
    m = jnp.mean(x, axis=axis, keepdims=True)
    v = jnp.var(x, axis=axis, keepdims=True)
    return (x - m) / jnp.sqrt(v + eps)

def _scatter_add(tgt, idx, src, axis=0):
    return tgt.at[idx].add(src)

def _segment_sum(src, seg, n):
    return jax.ops.segment_sum(src, seg, n)
kernel_name = 'mk_conv_preact_d2_conv_nchw256_r2_3cd123'

def setup_inputs(seed: int=0):
    np.random.seed(seed)
    _w = jnp.asarray

    def _rec_inputs():
        import jax
        import jax.numpy as jnp
        _gk = jax.random.key(seed)
        x = -0.0002928 + 1 * jax.random.normal(jax.random.fold_in(_gk, 1), (4, 128, 32, 32), jnp.float32)
        return x
    x = _rec_inputs()

    def _L0_conv_setup():
        import jax, jax.numpy as jnp
        import numpy as np
        GAMMA = 2
        EPS = 1e-08
        B, C, H, WID = (4, 128, 32, 32)
        key = jax.random.key(seed)
        kx, kw = jax.random.split(key)
        x = jax.random.normal(kx, (B, C, H, WID), dtype=jnp.float32)
        W = jax.random.normal(kw, (C, C), dtype=jnp.float32) * 0.02
        b = jnp.zeros((C,), dtype=jnp.float32)
        return {'x': x, 'W': W, 'b': b}
    _L0_conv_all = _L0_conv_setup()
    _L0_conv_in = {k: v for k, v in _L0_conv_all.items() if k in ('W', 'b')}
    del _L0_conv_all

    def _L1_conv_setup():
        import jax, jax.numpy as jnp
        import numpy as np

        def conv2d_same(x, w, b=None):
            out = jax.lax.conv_general_dilated(x, w, window_strides=(1, 1), padding='SAME', dimension_numbers=('NCHW', 'OIHW', 'NCHW'))
            if b is not None:
                out = out + b[None, :, None, None]
            return out

        def deform_conv(x, offset, wd, k=3, pad=1, dg=4):
            B, C, H, W = x.shape
            cg = C // dg
            K = k * k
            off = offset.reshape(B, dg, K, 2, H, W)
            dy, dx = (off[:, :, :, 0], off[:, :, :, 1])
            ky = (jnp.arange(K) // k - pad).astype(x.dtype)
            kx = (jnp.arange(K) % k - pad).astype(x.dtype)
            hh = jnp.arange(H, dtype=x.dtype)
            ww = jnp.arange(W, dtype=x.dtype)
            py = dy + ky[None, None, :, None, None] + hh[None, None, None, :, None]
            px = dx + kx[None, None, :, None, None] + ww[None, None, None, None, :]
            y0 = jnp.floor(py)
            x0 = jnp.floor(px)
            wy1 = py - y0
            wy0 = 1.0 - wy1
            wx1 = px - x0
            wx0 = 1.0 - wx1
            xg = x.reshape(B, dg, cg, H * W)

            def gather(yi, xi):
                valid = (yi >= 0) & (yi < H) & (xi >= 0) & (xi < W)
                yc = jnp.clip(yi, 0, H - 1).astype(jnp.int32)
                xc = jnp.clip(xi, 0, W - 1).astype(jnp.int32)
                idx = (yc * W + xc).reshape(B, dg, 1, K * H * W)
                g = jnp.take_along_axis(xg, jnp.broadcast_to(idx, (B, dg, cg, K * H * W)), axis=-1)
                g = g.reshape(B, dg, cg, K, H, W)
                return g * valid[:, :, None].astype(x.dtype)
            val = gather(y0, x0) * (wy0 * wx0)[:, :, None] + gather(y0, x0 + 1) * (wy0 * wx1)[:, :, None] + gather(y0 + 1, x0) * (wy1 * wx0)[:, :, None] + gather(y0 + 1, x0 + 1) * (wy1 * wx1)[:, :, None]
            wr = wd.reshape(wd.shape[0], dg, cg, K)
            return jnp.einsum('ogck,bgckhw->bohw', wr, val)
        key = jax.random.key(seed)
        k1, k2, k3, k4 = jax.random.split(key, 4)
        B, C, H, W = (8, 128, 32, 32)
        dg, ks = (4, 3)
        x = jax.random.normal(k1, (B, C, H, W), dtype=jnp.float32)
        w1 = jax.random.normal(k2, (C, C, 3, 3), dtype=jnp.float32) * 0.01
        b1 = jnp.zeros((C,), dtype=jnp.float32)
        w2 = jax.random.normal(k3, (dg * ks * ks * 2, C, 3, 3), dtype=jnp.float32) * 0.01
        b2 = jnp.zeros((dg * ks * ks * 2,), dtype=jnp.float32)
        wd = jax.random.normal(k4, (C, C, ks, ks), dtype=jnp.float32) * 0.01
        return {'x': x, 'w1': w1, 'b1': b1, 'w2': w2, 'b2': b2, 'wd': wd}
    _L1_conv_all = _L1_conv_setup()
    _L1_conv_in = {k: v for k, v in _L1_conv_all.items() if k in ('w1', 'b1', 'w2', 'b2', 'wd')}
    del _L1_conv_all
    return {'x': x, 'L0_conv_W': _L0_conv_in['W'], 'L0_conv_b': _L0_conv_in['b'], 'L1_conv_w1': _L1_conv_in['w1'], 'L1_conv_b1': _L1_conv_in['b1'], 'L1_conv_w2': _L1_conv_in['w2'], 'L1_conv_b2': _L1_conv_in['b2'], 'L1_conv_wd': _L1_conv_in['wd']}

def reference(x, L0_conv_W, L0_conv_b, L1_conv_w1, L1_conv_b1, L1_conv_w2, L1_conv_b2, L1_conv_wd):
    import jax
    import jax.numpy as jnp

    def _L0_conv_ref(x, W, b):
        import jax, jax.numpy as jnp
        import numpy as np
        GAMMA = 2
        EPS = 1e-08
        B, C, H, WID = (4, 128, 32, 32)
        Bs, Cs, Hs, Ws = x.shape
        xf = x.reshape(Bs, Cs, Hs * Ws)
        norm = jnp.sqrt(jnp.sum(xf * xf, axis=1, keepdims=True))
        xn = xf / jnp.maximum(norm, EPS)
        s = jax.nn.relu(jnp.einsum('bcp,bcq->bpq', xn, xn)) ** GAMMA
        gx = jnp.einsum('oc,bcp->bop', W, xf) + b[None, :, None]
        y = jnp.einsum('bpq,bcq->bcp', s, gx)
        return y.reshape(Bs, Cs, Hs, Ws)

    def _L1_conv_ref(x, w1, b1, w2, b2, wd):
        import jax, jax.numpy as jnp
        import numpy as np

        def conv2d_same(x, w, b=None):
            out = jax.lax.conv_general_dilated(x, w, window_strides=(1, 1), padding='SAME', dimension_numbers=('NCHW', 'OIHW', 'NCHW'))
            if b is not None:
                out = out + b[None, :, None, None]
            return out

        def deform_conv(x, offset, wd, k=3, pad=1, dg=4):
            B, C, H, W = x.shape
            cg = C // dg
            K = k * k
            off = offset.reshape(B, dg, K, 2, H, W)
            dy, dx = (off[:, :, :, 0], off[:, :, :, 1])
            ky = (jnp.arange(K) // k - pad).astype(x.dtype)
            kx = (jnp.arange(K) % k - pad).astype(x.dtype)
            hh = jnp.arange(H, dtype=x.dtype)
            ww = jnp.arange(W, dtype=x.dtype)
            py = dy + ky[None, None, :, None, None] + hh[None, None, None, :, None]
            px = dx + kx[None, None, :, None, None] + ww[None, None, None, None, :]
            y0 = jnp.floor(py)
            x0 = jnp.floor(px)
            wy1 = py - y0
            wy0 = 1.0 - wy1
            wx1 = px - x0
            wx0 = 1.0 - wx1
            xg = x.reshape(B, dg, cg, H * W)

            def gather(yi, xi):
                valid = (yi >= 0) & (yi < H) & (xi >= 0) & (xi < W)
                yc = jnp.clip(yi, 0, H - 1).astype(jnp.int32)
                xc = jnp.clip(xi, 0, W - 1).astype(jnp.int32)
                idx = (yc * W + xc).reshape(B, dg, 1, K * H * W)
                g = jnp.take_along_axis(xg, jnp.broadcast_to(idx, (B, dg, cg, K * H * W)), axis=-1)
                g = g.reshape(B, dg, cg, K, H, W)
                return g * valid[:, :, None].astype(x.dtype)
            val = gather(y0, x0) * (wy0 * wx0)[:, :, None] + gather(y0, x0 + 1) * (wy0 * wx1)[:, :, None] + gather(y0 + 1, x0) * (wy1 * wx0)[:, :, None] + gather(y0 + 1, x0 + 1) * (wy1 * wx1)[:, :, None]
            wr = wd.reshape(wd.shape[0], dg, cg, K)
            return jnp.einsum('ogck,bgckhw->bohw', wr, val)
        xd = jax.lax.stop_gradient(x)
        offset = conv2d_same(conv2d_same(xd, w1, b1), w2, b2)
        return jax.nn.relu(deform_conv(x, offset, wd, k=3, pad=1, dg=4))

    def _gn(v, G=32, eps=1e-05):
        B_, C_, H_, W_ = v.shape
        g = v.reshape(B_, G, C_ // G, H_, W_)
        m = jnp.mean(g, axis=(2, 3, 4), keepdims=True)
        s = jnp.var(g, axis=(2, 3, 4), keepdims=True)
        return ((g - m) / jnp.sqrt(s + eps)).reshape(v.shape)

    def _ln_c(v, eps=1e-06):
        m = jnp.mean(v, axis=1, keepdims=True)
        s = jnp.var(v, axis=1, keepdims=True)
        return (v - m) / jnp.sqrt(s + eps)

    def _ln_t(v, eps=1e-05):
        m = jnp.mean(v, axis=-1, keepdims=True)
        s = jnp.var(v, axis=-1, keepdims=True)
        return (v - m) / jnp.sqrt(s + eps)

    def _to_tokens(v):
        B_, C_, H_, W_ = v.shape
        return v.reshape(B_, C_, H_ * W_).transpose(0, 2, 1)

    def _from_tokens(t, like):
        B_, C_, H_, W_ = like.shape
        return t.transpose(0, 2, 1).reshape(B_, C_, H_, W_)
    x = x + _L0_conv_ref(_gn(x), L0_conv_W, L0_conv_b)
    x = x + _L1_conv_ref(_gn(x), L1_conv_w1, L1_conv_b1, L1_conv_w2, L1_conv_b2, L1_conv_wd)
    return x

_drawn_inputs = setup_inputs


def setup_inputs(seed=0):
    import zlib

    import numpy as np

    out = dict(_drawn_inputs(seed))
    spreads = {'L0_conv_b': (0.0, 0.1), 'L1_conv_b1': (0.0, 0.787), 'L1_conv_b2': (0.0, 0.268)}
    factors = {}
    for name, (base, spread) in spreads.items():
        noise = np.random.default_rng([zlib.crc32(name.encode()), seed]).standard_normal(out[name].shape)
        drawn = base * np.exp(spread * noise) if base else spread * noise
        out[name] = jnp.asarray(drawn.astype(out[name].dtype))
    for name, factor in factors.items():
        out[name] = (out[name] * factor).astype(out[name].dtype)
    return out
```

```python
from contextlib import ExitStack

import concourse.bass as bass
from concourse import mybir

F32 = mybir.dt.float32
I32 = mybir.dt.int32
ACT = mybir.ActivationFunctionType
ALU = mybir.AluOpType
AX = mybir.AxisListType

P = 128


def mix_deform_kernel(nc, x, W0, b0, w1, b1, w2, b2, wd, out):
    B, C, H, WID = x.shape
    NPIX = H * WID
    HALF = NPIX // 2
    G, K = 4, 9
    CG = C // G
    NOFF = 2 * G * K
    REACH = 2
    BLK = 4
    RIM = REACH + 1
    WIN = BLK + 2 * RIM
    CELLS = WIN * WIN
    SUP = BLK + 2 * REACH
    ROWT = H // BLK
    NBLK = WID // BLK
    BP = BLK * BLK
    HP = H + 2 * RIM
    CP = H + 2
    QT = NPIX // P
    GN_EPS, NORM_EPS = 1e-5, 1e-8
    BANK = 512
    TGROUPS = K + 2
    VGROUPS = ((0, 3), (3, 6), (6, 8))
    SLOTS = K * ROWT
    assert C == P and BLK * WID == P and G * CG == C and QT == 8 and ROWT == 8

    ctx = ExitStack()
    with ctx:
        def sb(name, shape, dt=F32):
            return ctx.enter_context(nc.sbuf_tensor(name, shape, dt))

        def pb(name, shape, dt=F32):
            return ctx.enter_context(nc.psum_tensor(name, shape, dt))

        def sem(name):
            return ctx.enter_context(nc.semaphore(name))

        ident = sb("ident", [P, P])
        ones = sb("ones", [P, P])
        avg4 = sb("avg4", [P, P])
        avg4b = sb("avg4b", [P, P])
        cell_idx = sb("cell_idx", [P, SUP])
        grid = sb("grid", [P, 2])
        grid_i = sb("grid_i", [P, 4], I32)
        block_col = sb("block_col", [P, 1])
        eps_col = sb("eps_col", [P, 1])
        w0_sb = sb("w0_sb", [P, C])
        w1_sb = sb("w1_sb", [P, K, C])
        w2_sb = sb("w2_sb", [P, K, NOFF])
        wd_sb = sb("wd_sb", [P, K, C])
        b0_row = sb("b0_row", [P, C])
        b1_col = sb("b1_col", [P, 1])
        b2_col = sb("b2_col", [NOFF, 1])
        x_all = sb("x_all", [P, B, NPIX])
        pos_all = sb("pos_all", [P, B, ROWT, NOFF])
        bn = sb("bn", [P, 2, 6])
        mv = sb("mv", [P, 2])
        dev = sb("dev", [P, 1])
        varp = sb("varp", [P, 1])
        mean = sb("mean", [P, 1])
        sd = sb("sd", [P, 1])
        rstd = sb("rstd", [P, 1])
        g_sb = sb("g_sb", [P, NPIX])
        sq = sb("sq", [P, NPIX])
        off_ch = sq[0:NOFF, :]
        nrm = sb("nrm", [P, NPIX])
        xn = sb("xn", [P, NPIX])
        gxT = sb("gxT", [P, QT, C])
        rel = sb("rel", [P, 2, NPIX])
        sim = sb("sim", [P, 2, NPIX])
        hpad = sb("hpad", [P, HP, HP])
        cpad = sb("cpad", [P, CP, CP])
        hcol = sb("hcol", [P, NBLK, HP, WIN])
        dist = sb("dist", [P, NOFF, SUP])
        fold = sb("fold", [P, NOFF, SUP])
        tent = sb("tent", [P, NOFF, SUP])
        wpix = sb("wpix", [P, 2, K, G, CELLS])
        wcell = sb("wcell", [CELLS, 2, K, G, P])
        hwin = sb("hwin", [CELLS, 2, NBLK, C])
        val = sb("val", [P, 4, NBLK, K * BP])
        extremes = sb("extremes", [NOFF, 2, B])
        ends = sb("ends", [NOFF, 2])
        farthest = sb("farthest", [NOFF, 1])
        far_all = sb("far_all", [1, 1])
        beyond = sb("beyond", [1, 1], I32)
        norm2nd = sb("norm2nd", [P, B, 2])
        cell32 = sb("cell32", [P, WID])
        tap_at = sb("tap_at", [P, K, 2])
        row_at = sb("row_at", [P, ROWT])
        stat_cur = sb("stat_cur", [P, 3])
        place = dist[:, 0:G * K * 2 // SUP, :].rearrange("p a b -> p (a b)")
        wide = wpix[:, 0, :, :, :].rearrange("p k g q -> p (k g q)")
        narrow = wpix[:, 1, :, :, :].rearrange("p k g q -> p (k g q)")
        GK = G * K
        tent_y, tent_x, wide_tmp = (wide[:, i * GK * WID:(i + 1) * GK * WID].rearrange("p (n r) -> p n r", r=WID)
                                    for i in range(3))
        plane = narrow[:, 0:G * P]
        plane_t = narrow[:, G * P:2 * G * P]
        h_cur = narrow[:, 2 * G * P:2 * G * P + C]
        acc = narrow[:, 2 * G * P + C:2 * G * P + C + K * P].rearrange("p (k n) -> p k n", k=K)
        orelu = sb("orelu", [P, 2, HALF])
        yout = sb("yout", [P, 2, HALF])

        psT = pb("psT", [P, 2, BANK])
        psV = pb("psV", [P, 2, BANK])
        psA = pb("psA", [P, 2, BANK])
        psB = pb("psB", [P, 2, BANK])

        s = {n: sem(n) for n in (
            "x_first_in x_rest_in weights_in zeroed const_ready "
            "stats_done moments mean_done dev_done varp_done var_done sd_done rstd_done "
            "g_done g2_done norm2_done norm_done clamp_done inv_done xn_done gx_done gxT_done "
            "simps_done rel_done sim_done mix_done x1_done h_done "
            "conv1_done cpad_done conv2_done off_done offT_done pos_done "
            "extremes_done ends_done farthest_done far_turned far_all_done flag_done coords_ready "
            "stat2_done g_stat g_h g_hT g_hTs g_place g_shift g_d1 g_f1 g_tent g_zero g_cur g_plane g_turn g_planeT "
            "g_sample g_acc g_conv g_relu g_out g_stored "
            "strips_done dist_done fold_done tent_done weights_done turned turn_free "
            "sampled val_free dconv_done orelu_done yout_done settled grid_ready out_first out_second").split()}
        out_sems = [s["out_first"], s["out_second"]]

        block = ctx.enter_context(nc.Block())

        def batch(ap, b):
            return ap[:, bass.ds(b, 1), :].rearrange("p b n -> p (b n)")

        SCORE = [10 + 4 * i for i in range(QT)]
        MIX = [13 + 4 * i for i in range(QT)]
        CONV1, CONV2 = 50, 60

        TURNED0, SAMPLED0, DCONV0 = 1, 4, 1

        def settle(eng):
            eng.sem_inc(s["settled"], 1)

        def is_beyond(eng):
            eng.wait_ge(s["flag_done"], 1)
            return eng.value_load(beyond[0:1, 0:1], min_val=0, max_val=1) > 0

        @block.sync
        def _(sp):
            sp.dma_start(x_all[:, 0, :], x[0].rearrange("c h w -> c (h w)")).then_inc(s["x_first_in"], 16)
            sp.dma_start(w0_sb[:, :], W0).then_inc(s["weights_in"], 16)
            sp.dma_start(b0_row[:, :], b0.partition_broadcast(P)).then_inc(s["weights_in"], 16)
            sp.dma_start(b1_col[:, :], b1).then_inc(s["weights_in"], 16)
            sp.dma_start(b2_col[:, :], b2).then_inc(s["weights_in"], 16)
            sp.dma_start(w1_sb[:, :, :], w1).then_inc(s["weights_in"], 16)
            sp.dma_start(w2_sb[:, :, :], w2).then_inc(s["weights_in"], 16)
            sp.dma_start(wd_sb[:, :, :], wd).then_inc(s["weights_in"], 16)
            sp.dma_start(x_all[:, 1:B, :], x[1:B].rearrange("b c h w -> c b (h w)")).then_inc(s["x_rest_in"], 16)
            for half in range(2):
                sp.nop().then_inc(out_sems[half], 16)
            sp.nop().then_inc(s["g_stored"], 16)
            with sp.Fori(0, B) as b:
                for half in range(2):
                    sp.wait_ge(s["yout_done"], 2 * b + half + 1)
                    rows = slice(half * H // 2, (half + 1) * H // 2)
                    sp.dma_start(out[bass.ds(b, 1), :, rows, :].rearrange("b c h w -> c (b h w)"),
                                 yout[:, half, :]).then_inc(out_sems[half], 16)
            for half in range(2):
                sp.wait_ge(out_sems[half], 16 * (B + 1))
            with sp.If(is_beyond(sp)):
                with sp.Fori(0, B) as b:
                    with sp.Fori(0, ROWT) as t:
                        sp.wait_ge(s["g_out"], ROWT * b + t + 1)
                        sp.dma_start(out[bass.ds(b, 1), :, bass.ds(BLK * t, BLK), :].rearrange("b c h w -> c (b h w)"),
                                     yout[:, 0, 0:P]).then_inc(s["g_stored"], 16)
                sp.wait_ge(s["g_stored"], 16 * (B * ROWT + 1))

        @block.gpsimd
        def _(pool):
            def chain(k):
                pool.wait_ge(s["zeroed"], k)

            pool.memset(ident[:, :], 0.0).then_inc(s["zeroed"], 1)
            pool.memset(avg4[:, :], 1.0 / 4).then_inc(s["zeroed"], 1)
            pool.memset(hpad[:, :, :], 0.0).then_inc(s["zeroed"], 1)
            pool.memset(cpad[:, :, :], 0.0).then_inc(s["zeroed"], 1)
            pool.memset(wpix[:, :, :, :, :], 0.0).then_inc(s["zeroed"], 1)
            pool.memset(ones[:, :], 1.0).then_inc(s["zeroed"], 1)
            pool.memset(eps_col[:, :], GN_EPS).then_inc(s["zeroed"], 1)
            pool.iota(cell_idx[:, :], [[1, SUP]], base=0, channel_multiplier=0,
                      allow_small_or_imprecise_dtypes=True).then_inc(s["zeroed"], 1)
            pool.iota(grid_i[:, 0:1], [[0, 1]], base=0, channel_multiplier=1).then_inc(s["zeroed"], 1)
            chain(9)
            pool.iota(cell32[:, :], [[1, WID]], base=0, channel_multiplier=0,
                      allow_small_or_imprecise_dtypes=True).then_inc(s["coords_ready"], 1)
            pool.iota(row_at[:, :], [[BLK, ROWT]], base=0, channel_multiplier=0,
                      allow_small_or_imprecise_dtypes=True).then_inc(s["coords_ready"], 1)
            pool.iota(tap_at[:, :, 0:1].rearrange("p (a b) o -> p a (b o)", a=3), [[1, 3], [0, 3]], base=-RIM,
                      channel_multiplier=0, allow_small_or_imprecise_dtypes=True).then_inc(s["coords_ready"], 1)
            pool.iota(tap_at[:, :, 1:2].rearrange("p (a b) o -> p a (b o)", a=3), [[0, 3], [1, 3]], base=-RIM,
                      channel_multiplier=0, allow_small_or_imprecise_dtypes=True).then_inc(s["coords_ready"], 1)
            pool.affine_select(out=ident[:, :], in_=ident[:, :], compare_op=ALU.not_equal, fill=1.0,
                               base=0, pattern=[[-1, P]], channel_multiplier=1).then_inc(s["const_ready"], 1)
            a4 = avg4[:, :].rearrange("p (j r) -> p j r", r=4)
            a4b = avg4b[:, :].rearrange("p (j r) -> p j r", r=4)
            pool.affine_select(out=a4b, in_=a4, compare_op=ALU.is_ge, fill=0.0, base=0,
                               pattern=[[-4, P // 4], [0, 4]], channel_multiplier=1).then_inc(s["const_ready"], 1)
            pool.wait_ge(s["const_ready"], 2)
            pool.affine_select(out=a4, in_=a4b, compare_op=ALU.is_ge, fill=0.0, base=3,
                               pattern=[[4, P // 4], [0, 4]], channel_multiplier=-1).then_inc(s["const_ready"], 1)

            def front(b):
                for i in range(QT):
                    pool.wait_ge(s["rel_done"], 2 * QT * b + 2 * i + 2)
                    if i >= 2:
                        pool.wait_ge(s["mix_done"], QT * b + i - 1)
                    pool.tensor_tensor(sim[:, i % 2, :], rel[:, i % 2, :], rel[:, i % 2, :],
                                       ALU.mult).then_inc(s["sim_done"], 1)

            def strips(b):
                pool.wait_ge(s["h_done"], b + 1)
                settle(pool)
                for u in range(NBLK):
                    pool.tensor_copy(hcol[:, u, :, :], hpad[:, :, BLK * u:BLK * u + WIN])\
                        .then_inc(s["strips_done"], 1)

            front(0)
            strips(0)
            with pool.Fori(0, B - 1) as b:
                front(b + 1)
                pool.wait_ge(s["turned"], (b + 1) * ROWT * TGROUPS + TURNED0)
                strips(b + 1)

        @block.tensor
        def _(pe):
            def group_mean(b, second, col):
                if col == 0:
                    pe.wait_ge(s["moments"], 2 * b + second + 1)
                    src = mv[:, 0:1]
                else:
                    pe.wait_ge(s["varp_done"], 2 * b + second + 1)
                    src = varp[:, :]
                pe.matmul(psB[:, 0, col:col + 1], avg4[:, :], src, start=True, stop=True)\
                    .then_inc(s["mean_done" if col == 0 else "var_done"], 1)

            def gx(b):
                pe.wait_ge(s["g_done"], b + 1)
                for i in range(QT):
                    last = pe.matmul(psA[:, i // 4, (i % 4) * C:(i % 4 + 1) * C],
                                     g_sb[:, i * P:(i + 1) * P], w0_sb[:, :], start=True, stop=True)
                last.then_inc(s["gx_done"], 1)

            def norm2(b):
                pe.wait_ge(s["g2_done"], b + 1)
                for j in range(2):
                    last = pe.matmul(psB[:, j, :], ones[:, :], sq[:, j * HALF:(j + 1) * HALF], start=True, stop=True)
                last.then_inc(s["norm2_done"], 1)

            def score(b, i):
                if i == 0:
                    pe.wait_ge(s["xn_done"], b + 1)
                for j in range(2):
                    if i >= 1:
                        pe.wait_ge(s["rel_done"], 2 * QT * b + 2 * (i - 1) + j + 1)
                    pe.matmul(psB[:, j, :], xn[:, i * P:(i + 1) * P], xn[:, j * HALF:(j + 1) * HALF],
                              start=True, stop=True).then_inc(s["simps_done"], 1)

            def mix(b, i):
                if i == 0:
                    pe.wait_ge(s["gxT_done"], b + 1)
                pe.wait_ge(s["sim_done"], QT * b + i + 1)
                for j in range(2):
                    last = pe.matmul(psA[:, j, :], gxT[:, i, :], sim[:, i % 2, j * HALF:(j + 1) * HALF],
                                     start=(i == 0), stop=(i == QT - 1))
                last.then_inc(s["mix_done"], 1)

            def conv1(b, k):
                if k == 0:
                    pe.wait_ge(s["h_done"], b + 1)
                ky, kx = divmod(k, 3)
                for j in range(2):
                    r = RIM - 1 + ky + j * H // 2
                    last = pe.matmul(psA[:, j, :], w1_sb[:, k, :],
                                     hpad[:, r:r + H // 2, RIM - 1 + kx:RIM - 1 + kx + WID],
                                     start=(k == 0), stop=(k == K - 1))
                if k == K - 1:
                    last.then_inc(s["conv1_done"], 1)

            def conv2(b, k):
                if k == 0:
                    pe.wait_ge(s["cpad_done"], 2 * b + 2)
                ky, kx = divmod(k, 3)
                for j in range(2):
                    r = ky + j * H // 2
                    last = pe.matmul(psB[0:NOFF, j, :], w2_sb[:, k, :],
                                     cpad[:, r:r + H // 2, kx:kx + WID],
                                     start=(k == 0), stop=(k == K - 1))
                if k == K - 1:
                    last.then_inc(s["conv2_done"], 1)

            def turn_offsets(b):
                pe.wait_ge(s["off_done"], 2 * b + 2)
                for t in range(ROWT):
                    last = pe.transpose(psA[:, t // 4, (t % 4) * NOFF:(t % 4 + 1) * NOFF],
                                        off_ch[:, t * P:(t + 1) * P], ident[0:NOFF, 0:NOFF])
                last.then_inc(s["offT_done"], 1)

            def front(b, n):
                if n in (1, 43):
                    group_mean(b, int(n == 43), 0)
                if n in (2, 44):
                    group_mean(b, int(n == 44), 1)
                if n == 5:
                    gx(b)
                if n == 6:
                    norm2(b)
                if n in SCORE:
                    score(b, SCORE.index(n))
                if n in MIX:
                    mix(b, MIX.index(n))
                if CONV1 <= n < CONV1 + K:
                    conv1(b, n - CONV1)
                if CONV2 <= n < CONV2 + K:
                    conv2(b, n - CONV2)
                if n == SLOTS - 1:
                    turn_offsets(b)

            def turns(b, t, k):
                n = TGROUPS * t + k
                pe.wait_ge(s["turn_free"], TGROUPS * ROWT * b + n + 1)
                return psT[:, n % 2, :]

            def cut_windows(b, t):
                if t == 0:
                    pe.wait_ge(s["strips_done"], NBLK * (b + 1))
                for k in range(2):
                    bank = turns(b, t, k)
                    for v in range(4):
                        u = 4 * k + v
                        strip = hcol[:, u, BLK * t:BLK * t + WIN, :].rearrange("p r c -> p (r c)")
                        last = pe.transpose(bank[0:CELLS, v * C:(v + 1) * C], strip, ident[:, :])
                    last.then_inc(s["turned"], 1)

            def turn_weights(b, t, k):
                pe.wait_ge(s["weights_done"], K * ROWT * b + K * t + k + 1)
                bank = turns(b, t, 2 + k)
                for g in range(G):
                    last = pe.transpose(bank[0:CELLS, g * P:(g + 1) * P], wpix[:, t % 2, k, g, :], ident[:, :])
                last.then_inc(s["turned"], 1)

            def sample(b, t, u):
                v = [i for i, (lo, hi) in enumerate(VGROUPS) if lo <= u < hi][0]
                n = len(VGROUPS) * t + v
                lo, hi = VGROUPS[v]
                if u == 0:
                    pe.wait_ge(s["turn_free"], TGROUPS * ROWT * b + TGROUPS * (t + 1) + 2)
                if u == lo:
                    pe.wait_ge(s["val_free"], len(VGROUPS) * ROWT * b + n + 1)
                for g in range(G):
                    w = wcell[:, t % 2, :, g, :].rearrange("q k (i c) -> q k i c", i=BLK)
                    last = pe.matmul(psV[g * CG:(g + 1) * CG, n % 2, (u - lo) * K * BP:(u - lo + 1) * K * BP],
                                     hwin[:, t % 2, u, g * CG:(g + 1) * CG],
                                     w[:, :, :, BLK * u:BLK * (u + 1)], start=True, stop=True)
                if u == hi - 1:
                    last.then_inc(s["sampled"], 1)

            def dconv(b, half):
                pe.wait_ge(s["val_free"], len(VGROUPS) * (ROWT * b + 4 * (half + 1)) + 2)
                v = val[:, :, :, :].rearrange("p t u n -> p (t u) n")
                for k in range(K):
                    last = pe.matmul(psB[:, 1, :], wd_sb[:, k, :], v[:, :, k * BP:(k + 1) * BP],
                                     start=(k == 0), stop=(k == K - 1))
                last.then_inc(s["dconv_done"], 1)

            def turn_farthest():
                pe.wait_ge(s["farthest_done"], 1)
                pe.transpose(psA[0:1, 0, 0:NOFF], farthest[:, :], ident[0:NOFF, 0:NOFF]).then_inc(s["far_turned"], 1)

            def general_path():
                with pe.Fori(0, B) as b:
                    pe.wait_ge(s["g_h"], b + 1)
                    for i in range(QT):
                        last = pe.transpose(psT[:, i // 4, (i % 4) * C:(i % 4 + 1) * C],
                                            g_sb[:, i * P:(i + 1) * P], ident[:, :])
                    last.then_inc(s["g_hT"], 1)
                    with pe.Fori(0, ROWT) as t:
                        with pe.Fori(0, QT) as m:
                            for k in range(K):
                                n = K * (QT * (ROWT * b + t) + m) + k
                                pe.wait_ge(s["g_plane"], n + 1)
                                for g in range(G):
                                    last = pe.transpose(psA[:, 0, g * P:(g + 1) * P],
                                                        plane[:, g * P:(g + 1) * P], ident[:, :])
                                last.then_inc(s["g_turn"], 1)
                                pe.wait_ge(s["g_planeT"], n + 1)
                                for g in range(G):
                                    last = pe.matmul(psV[g * CG:(g + 1) * CG, 0, 0:P], h_cur[:, g * CG:(g + 1) * CG],
                                                     plane_t[:, g * P:(g + 1) * P], start=True, stop=True)
                                last.then_inc(s["g_sample"], 1)
                        pe.wait_ge(s["g_acc"], K * QT * (ROWT * b + t + 1))
                        for k in range(K):
                            last = pe.matmul(psB[:, 1, 0:P], wd_sb[:, k, :], acc[:, k, :],
                                             start=(k == 0), stop=(k == K - 1))
                        last.then_inc(s["g_conv"], 1)

            def batch_steps(b, nxt):
                if nxt is None:
                    turn_farthest()
                for t in range(ROWT + 1):
                    if t < ROWT:
                        cut_windows(b, t)
                    for k in range(K):
                        if t < ROWT:
                            turn_weights(b, t, k)
                        if t >= 1 and k < NBLK:
                            sample(b, t - 1, k)
                        if t == 5 and k == 1:
                            dconv(b, 0)
                        if nxt is not None and t < ROWT:
                            front(nxt, K * t + k)
                dconv(b, 1)

            pe.nop().then_inc(s["turned"], TURNED0)
            pe.nop().then_inc(s["g_sample"], 1)
            pe.nop().then_inc(s["sampled"], SAMPLED0)
            pe.nop().then_inc(s["dconv_done"], DCONV0)
            pe.wait_ge(s["const_ready"], 3)
            pe.wait_ge(s["zeroed"], 9)
            pe.wait_ge(s["weights_in"], 7 * 16)
            for n in range(SLOTS):
                front(0, n)
            with pe.Fori(0, B - 1) as b:
                batch_steps(b, b + 1)
            batch_steps(B - 1, None)
            with pe.If(is_beyond(pe)):
                general_path()

        @block.scalar
        def _(act):
            def std(b, second):
                act.wait_ge(s["var_done"], 2 * b + second + 1)
                act.activation(sd[:, :], psB[:, 0, 1:2], ACT.Sqrt, bias=eps_col[:, :]).then_inc(s["sd_done"], 1)

            def front(b, n):
                if n in (2, 44):
                    std(b, int(n == 44))
                if n == 4:
                    act.wait_ge(s["g_done"], b + 1)
                    act.activation(sq[:, :], g_sb[:, :], ACT.Square).then_inc(s["g2_done"], 1)
                if n == 7:
                    act.wait_ge(s["norm2_done"], b + 1)
                    act.activation(nrm[:, :], psB[:, :, :].rearrange("p j n -> p (j n)"), ACT.Sqrt)\
                        .then_inc(s["norm_done"], 1)
                if n in SCORE:
                    i = SCORE.index(n)
                    for j in range(2):
                        act.wait_ge(s["simps_done"], 2 * QT * b + 2 * i + j + 1)
                        if i >= 2 and j == 0:
                            act.wait_ge(s["sim_done"], QT * b + i - 1)
                        act.activation(rel[:, i % 2, j * HALF:(j + 1) * HALF], psB[:, j, :], ACT.Relu)\
                            .then_inc(s["rel_done"], 1)
                if n == CONV1 + K - 1:
                    act.wait_ge(s["conv1_done"], b + 1)
                    for j in range(2):
                        act.activation(cpad[:, 1 + j * H // 2:1 + (j + 1) * H // 2, 1:1 + WID],
                                       psA[:, j, :].rearrange("p (h w) -> p h w", w=WID),
                                       ACT.Identity, bias=b1_col[:, :]).then_inc(s["cpad_done"], 1)
                if n == CONV2 + K - 1:
                    act.wait_ge(s["conv2_done"], b + 1)
                    for j in range(2):
                        act.activation(off_ch[:, j * HALF:(j + 1) * HALF], psB[0:NOFF, j, :],
                                       ACT.Identity, bias=b2_col[:, :]).then_inc(s["off_done"], 1)

            def evacuate(b, t, k):
                n = TGROUPS * t + k
                if k == 0:
                    act.wait_ge(s["sampled"], len(VGROUPS) * (ROWT * b + t - 1) + SAMPLED0)
                act.wait_ge(s["turned"], TGROUPS * ROWT * b + n + 1 + TURNED0)
                if k < 2:
                    dst = hwin[:, t % 2, 4 * k:4 * k + 4, :].rearrange("q u c -> q (u c)")
                else:
                    dst = wcell[:, t % 2, k - 2, :, :].rearrange("q g p -> q (g p)")
                act.activation(dst, psT[0:CELLS, n % 2, :], ACT.Copy).then_inc(s["turn_free"], 1)

            def relu_out(b, half):
                act.wait_ge(s["dconv_done"], 2 * b + half + 1 + DCONV0)
                for t in range(4):
                    src = psB[:, 1, t * P:(t + 1) * P].rearrange("p (u i j) -> p u i j", u=NBLK, i=BLK)
                    dst = orelu[:, half, t * P:(t + 1) * P].rearrange("p (i u j) -> p u i j", u=NBLK, i=BLK)
                    last = act.activation(dst, src, ACT.Relu)
                last.then_inc(s["orelu_done"], 1)

            def general_path():
                with act.Fori(0, B) as b:
                    act.wait_ge(s["g_hT"], b + 1)
                    act.activation(gxT[:, :, :].rearrange("p i c -> p (i c)"),
                                   psT[:, :, :].rearrange("p j n -> p (j n)"), ACT.Copy).then_inc(s["g_hTs"], 1)
                    act.wait_ge(s["g_hTs"], b + 1)
                    settle(act)
                    with act.Fori(0, ROWT) as t:
                        with act.Fori(0, QT) as m:
                            turn = K * (QT * (ROWT * b + t) + m)
                            act.wait_ge(s["g_sample"], turn + 1)
                            settle(act)
                            act.activation(h_cur, gxT[:, bass.ds(m, 1), :].rearrange("p i c -> p (i c)"), ACT.Copy)\
                                .then_inc(s["g_cur"], 1)
                            for k in range(K):
                                act.wait_ge(s["g_turn"], turn + k + 1)
                                act.activation(plane_t, psA[:, 0, :], ACT.Copy).then_inc(s["g_planeT"], 1)
                        act.wait_ge(s["g_conv"], ROWT * b + t + 1)
                        act.activation(orelu[:, 0, 0:P], psB[:, 1, 0:P], ACT.Relu).then_inc(s["g_relu"], 1)

            def batch_steps(b, nxt):
                for t in range(ROWT + 1):
                    for k in range(K):
                        if t < ROWT:
                            if k == 0:
                                evacuate(b, t, 0)
                                evacuate(b, t, 1)
                            evacuate(b, t, 2 + k)
                        if t == 5 and k == 1:
                            relu_out(b, 0)
                        if nxt is not None and t < ROWT:
                            front(nxt, K * t + k)
                relu_out(b, 1)

            act.nop().then_inc(s["turn_free"], 2)
            act.wait_ge(s["zeroed"], 9)
            act.wait_ge(s["weights_in"], 7 * 16)
            for n in range(SLOTS):
                front(0, n)
            with act.Fori(0, B - 1) as b:
                batch_steps(b, b + 1)
            batch_steps(B - 1, None)
            with act.If(is_beyond(act)):
                general_path()

        @block.vector
        def _(dve):
            def channel_stats(b, second):
                n = 2 * b + second
                settle(dve)
                for j in range(2):
                    dve.bn_stats(bn[:, j, :], batch(x_all, b)[:, j * HALF:(j + 1) * HALF])\
                        .then_inc(s["stats_done"], 1)
                dve.wait_ge(s["stats_done"], 2 * n + 2)
                settle(dve)
                dve.bn_aggr(mv[:, :], bn[:, :, :]).then_inc(s["moments"], 1)

            def spread(b, second):
                n = 2 * b + second
                dve.wait_ge(s["moments"], n + 1)
                dve.wait_ge(s["mean_done"], n + 1)
                dve.tensor_copy(mean[:, :], psB[:, 0, 0:1]).then_inc(s["dev_done"], 1)
                dve.tensor_tensor(dev[:, :], mv[:, 0:1], psB[:, 0, 0:1], ALU.subtract).then_inc(s["dev_done"], 1)
                dve.wait_ge(s["dev_done"], 2 * n + 2)
                dve.scalar_tensor_tensor(out=varp[:, :], in0=dev[:, :], scalar=dev[:, :], in1=mv[:, 1:2],
                                         op0=ALU.mult, op1=ALU.add).then_inc(s["varp_done"], 1)

            def normalise(b, second):
                n = 2 * b + second
                dve.wait_ge(s["sd_done"], n + 1)
                dve.reciprocal(rstd[:, :], sd[:, :]).then_inc(s["rstd_done"], 1)
                dve.wait_ge(s["rstd_done"], n + 1)
                src = batch(x_all, b)
                if second:
                    dve.tensor_scalar(hpad[:, RIM:RIM + H, RIM:RIM + WID],
                                      src.rearrange("p (h w) -> p h w", w=WID), mean[:, :], rstd[:, :],
                                      ALU.subtract, ALU.mult).then_inc(s["h_done"], 1)
                else:
                    dve.tensor_scalar(g_sb[:, :], src, mean[:, :], rstd[:, :], ALU.subtract, ALU.mult)\
                        .then_inc(s["g_done"], 1)

            def front(b, n):
                if n == 0:
                    channel_stats(b, 0)
                if n in (1, 43):
                    spread(b, int(n == 43))
                if n == 3:
                    normalise(b, 0)
                if n == 5:
                    dve.wait_ge(s["gx_done"], b + 1)
                    dve.tensor_tensor(gxT[:, :, :], psA[:, :, :].rearrange("p j (i c) -> p (j i) c", c=C),
                                      b0_row[:, :].unsqueeze(1).to_broadcast([P, QT, C]),
                                      ALU.add).then_inc(s["gxT_done"], 1)
                if n == 8:
                    dve.wait_ge(s["norm_done"], b + 1)
                    dve.tensor_scalar(nrm[:, :], nrm[:, :], NORM_EPS, None, ALU.max).then_inc(s["clamp_done"], 1)
                    dve.wait_ge(s["clamp_done"], b + 1)
                    dve.reciprocal(nrm[:, :], nrm[:, :]).then_inc(s["inv_done"], 1)
                    dve.wait_ge(s["inv_done"], b + 1)
                    dve.tensor_tensor(xn[:, :], g_sb[:, :], nrm[:, :], ALU.mult).then_inc(s["xn_done"], 1)
                if n == 42:
                    dve.wait_ge(s["mix_done"], QT * (b + 1))
                    xb = batch(x_all, b)
                    dve.tensor_tensor(xb, xb, psA[:, :, :].rearrange("p j n -> p (j n)"), ALU.add)\
                        .then_inc(s["x1_done"], 1)
                    dve.wait_ge(s["x1_done"], b + 1)
                    channel_stats(b, 1)
                if n == 45:
                    normalise(b, 1)
                    for i, col in enumerate((mean, rstd)):
                        dve.tensor_copy(norm2nd[:, bass.ds(b, 1), i:i + 1].rearrange("p b i -> p (b i)"), col[:, :])\
                            .then_inc(s["stat2_done"], 1)
                if n == SLOTS - 1:
                    dve.wait_ge(s["offT_done"], b + 1)
                    for j in range(2):
                        src = psA[:, j, 0:4 * NOFF].rearrange("p (n a) -> p n a", a=2)
                        dst = pos_all[:, bass.ds(b, 1), 4 * j:4 * j + 4, :].rearrange("p b t (n a) -> p (b t n) a", a=2)
                        dve.tensor_tensor(dst, src, grid[:, :].unsqueeze(1).to_broadcast([P, 4 * NOFF // 2, 2]),
                                          ALU.add).then_inc(s["pos_done"], 1)
                    for i, op in enumerate((ALU.max, ALU.min)):
                        dve.tensor_reduce(extremes[:, i, bass.ds(b, 1)], off_ch, AX.X, op)\
                            .then_inc(s["extremes_done"], 1)

            def tents(b, t):
                n = ROWT * b + t
                if t == 0:
                    dve.wait_ge(s["pos_done"], 2 * b + 2)
                p = pos_all[:, bass.ds(b, 1), t, :].rearrange("p b n -> p (b n)")
                dve.tensor_tensor(dist[:, :, :], p.unsqueeze(2).to_broadcast([P, NOFF, SUP]),
                                  cell_idx[:, :].unsqueeze(1).to_broadcast([P, NOFF, SUP]),
                                  ALU.subtract).then_inc(s["dist_done"], 1)
                dve.wait_ge(s["dist_done"], n + 1)
                dve.scalar_tensor_tensor(out=fold[:, :, :], in0=dist[:, :, :], scalar=-1.0, in1=dist[:, :, :],
                                         op0=ALU.mult, op1=ALU.min).then_inc(s["fold_done"], 1)
                dve.wait_ge(s["fold_done"], n + 1)
                dve.tensor_scalar(tent[:, :, :], fold[:, :, :], 1.0, 0.0, ALU.add, ALU.max)\
                    .then_inc(s["tent_done"], 1)

            def weights(b, t, k):
                if k == 0:
                    tents(b, t)
                    dve.wait_ge(s["tent_done"], ROWT * b + t + 1)
                    if not (isinstance(b, int) and ROWT * b + t < 2):
                        dve.wait_ge(s["turned"], TGROUPS * (ROWT * b + t - 1) + TURNED0)
                ky, kx = divmod(k, 3)
                tv = tent[:, :, :].rearrange("p (g k a) r -> p g k a r", g=G, a=2)
                ty = tv[:, :, k, 0, :].unsqueeze(3).to_broadcast([P, G, SUP, SUP])
                tx = tv[:, :, k, 1, :].unsqueeze(2).to_broadcast([P, G, SUP, SUP])
                w = wpix[:, t % 2, k, :, :].rearrange("p g (r c) -> p g r c", c=WIN)
                dve.tensor_tensor(w[:, :, ky:ky + SUP, kx:kx + SUP], ty, tx, ALU.mult)\
                    .then_inc(s["weights_done"], 1)

            def take_samples(b, t, v):
                n = len(VGROUPS) * t + v
                lo, hi = VGROUPS[v]
                dve.wait_ge(s["sampled"], len(VGROUPS) * ROWT * b + n + 1 + SAMPLED0)
                if v == 0 and t % 4 == 0:
                    dve.wait_ge(s["dconv_done"], 2 * b + t // 4 + DCONV0)
                dve.tensor_copy(val[:, t % 4, lo:hi, :].rearrange("p u n -> p (u n)"),
                                psV[:, n % 2, 0:(hi - lo) * K * BP]).then_inc(s["val_free"], 1)

            def add_out(b, half):
                dve.wait_ge(s["orelu_done"], 2 * b + half + 1)
                dve.wait_ge(out_sems[half], 16 * b + 16)
                dve.tensor_tensor(yout[:, half, :], orelu[:, half, :],
                                  batch(x_all, b)[:, half * HALF:(half + 1) * HALF], ALU.add)\
                    .then_inc(s["yout_done"], 1)

            def find_farthest():
                dve.wait_ge(s["extremes_done"], 2 * B)
                dve.tensor_reduce(ends[:, 0:1], extremes[:, 0, :], AX.X, ALU.max).then_inc(s["ends_done"], 1)
                dve.tensor_reduce(ends[:, 1:2], extremes[:, 1, :], AX.X, ALU.min).then_inc(s["ends_done"], 1)
                dve.wait_ge(s["ends_done"], 2)
                dve.scalar_tensor_tensor(out=farthest[:, :], in0=ends[:, 1:2], scalar=-1.0, in1=ends[:, 0:1],
                                         op0=ALU.mult, op1=ALU.max).then_inc(s["farthest_done"], 1)
                dve.wait_ge(s["far_turned"], 1)
                dve.tensor_reduce(far_all[:, :], psA[0:1, 0, 0:NOFF], AX.X, ALU.max).then_inc(s["far_all_done"], 1)
                dve.wait_ge(s["far_all_done"], 1)
                dve.tensor_scalar(beyond[:, :], far_all[:, :], float(REACH), None, ALU.is_gt)\
                    .then_inc(s["flag_done"], 1)

            def general_tents(b, t):
                n = ROWT * b + t
                pos = pos_all[:, bass.ds(b, 1), bass.ds(t, 1), :].rearrange("p b t n -> p (b t n)")
                dve.tensor_tensor(place.rearrange("p (g k a) -> p g k a", g=G, a=2),
                                  pos.rearrange("p (g k a) -> p g k a", g=G, a=2),
                                  tap_at[:, :, :].unsqueeze(1).to_broadcast([P, G, K, 2]),
                                  ALU.add).then_inc(s["g_place"], 1)
                dve.tensor_copy(stat_cur[:, 2:3], row_at[:, bass.ds(t, 1)]).then_inc(s["g_place"], 1)
                dve.wait_ge(s["g_place"], 2 * n + 2)
                by_axis = place.rearrange("p (n a) -> p n a", a=2)
                rows = by_axis[:, :, 0:1].rearrange("p n o -> p (n o)")
                dve.tensor_scalar(rows, rows, stat_cur[:, 2:3], None, ALU.add).then_inc(s["g_shift"], 1)
                dve.wait_ge(s["g_shift"], n + 1)
                for a, dst in enumerate((tent_y, tent_x)):
                    m = 2 * n + a + 1
                    dve.tensor_tensor(wide_tmp, by_axis[:, :, a:a + 1].to_broadcast([P, GK, WID]),
                                      cell32[:, :].unsqueeze(1).to_broadcast([P, GK, WID]),
                                      ALU.subtract).then_inc(s["g_d1"], 1)
                    dve.wait_ge(s["g_d1"], m)
                    dve.scalar_tensor_tensor(out=dst, in0=wide_tmp, scalar=-1.0, in1=wide_tmp,
                                             op0=ALU.mult, op1=ALU.min).then_inc(s["g_f1"], 1)
                    dve.wait_ge(s["g_f1"], m)
                    dve.tensor_scalar(dst, dst, 1.0, 0.0, ALU.add, ALU.max).then_inc(s["g_tent"], 1)
                dve.memset(acc, 0.0).then_inc(s["g_zero"], 1)
                dve.wait_ge(s["g_tent"], 2 * n + 2)
                dve.wait_ge(s["g_zero"], n + 1)
                settle(dve)

            def general_path():
                dve.wait_ge(out_sems[0], 16 * (B + 1))
                dve.wait_ge(s["stat2_done"], 2 * B)
                with dve.Fori(0, B) as b:
                    dve.tensor_copy(stat_cur[:, 0:2], norm2nd[:, bass.ds(b, 1), :].rearrange("p b i -> p (b i)"))\
                        .then_inc(s["g_stat"], 1)
                    dve.wait_ge(s["g_stat"], b + 1)
                    dve.tensor_scalar(g_sb[:, :], batch(x_all, b), stat_cur[:, 0:1], stat_cur[:, 1:2],
                                      ALU.subtract, ALU.mult).then_inc(s["g_h"], 1)
                    with dve.Fori(0, ROWT) as t:
                        general_tents(b, t)
                        with dve.Fori(0, QT) as m:
                            for k in range(K):
                                n = K * (QT * (ROWT * b + t) + m) + k
                                ty = tent_y.rearrange("p (g k) r -> p g k r", g=G)[:, :, k, bass.ds(BLK * m, BLK)]
                                tx = tent_x.rearrange("p (g k) c -> p g k c", g=G)[:, :, k, :]
                                dve.tensor_tensor(plane.rearrange("p (g r c) -> p g r c", g=G, r=BLK),
                                                  ty.unsqueeze(3).to_broadcast([P, G, BLK, WID]),
                                                  tx.unsqueeze(2).to_broadcast([P, G, BLK, WID]),
                                                  ALU.mult).then_inc(s["g_plane"], 1)
                                dve.wait_ge(s["g_sample"], n + 1 + 1)
                                dve.tensor_tensor(acc[:, k, :], acc[:, k, :], psV[:, 0, 0:P], ALU.add)\
                                    .then_inc(s["g_acc"], 1)
                        n = ROWT * b + t
                        dve.wait_ge(s["g_relu"], n + 1)
                        dve.wait_ge(s["g_stored"], 16 * (n + 1))
                        dve.tensor_tensor(yout[:, 0, 0:P], orelu[:, 0, 0:P],
                                          batch(x_all, b)[:, bass.ds(P * t, P)], ALU.add)\
                            .then_inc(s["g_out"], 1)

            def batch_steps(b, nxt):
                if nxt is None:
                    find_farthest()
                for t in range(ROWT + 1):
                    for k in range(K):
                        if t < ROWT - 1:
                            weights(b, t + 1, k)
                        if t == ROWT and nxt is not None:
                            weights(nxt, 0, k)
                        if t >= 1 and k in (2, 5, 7):
                            take_samples(b, t - 1, (2, 5, 7).index(k))
                        if t == 5 and k == 2:
                            add_out(b, 0)
                        if nxt is not None and t < ROWT:
                            front(nxt, K * t + k)
                add_out(b, 1)

            dve.nop().then_inc(s["val_free"], 2)
            dve.wait_ge(s["zeroed"], 9)
            dve.tensor_scalar(grid_i[:, 1:2], grid_i[:, 0:1], 5, None, ALU.arith_shift_right)\
                .then_inc(s["grid_ready"], 1)
            dve.tensor_scalar(grid_i[:, 2:3], grid_i[:, 0:1], BLK - 1, None, ALU.bitwise_and)\
                .then_inc(s["grid_ready"], 1)
            dve.wait_ge(s["grid_ready"], 2)
            dve.tensor_scalar(grid[:, :], grid_i[:, 1:3], float(REACH), None, ALU.add).then_inc(s["grid_ready"], 1)
            dve.wait_ge(s["grid_ready"], 3)
            dve.tensor_scalar(grid_i[:, 3:4], grid_i[:, 0:1], WID - BLK, None, ALU.bitwise_and)\
                .then_inc(s["grid_ready"], 1)
            dve.wait_ge(s["grid_ready"], 4)
            dve.tensor_copy(block_col[:, :], grid_i[:, 3:4]).then_inc(s["grid_ready"], 1)
            dve.wait_ge(s["grid_ready"], 5)
            dve.wait_ge(s["coords_ready"], 4)
            dve.tensor_scalar(tap_at[:, :, 1:2], tap_at[:, :, 1:2], block_col[:, :], None, ALU.add)\
                .then_inc(s["grid_ready"], 1)
            dve.wait_ge(s["weights_in"], 7 * 16)
            dve.wait_ge(s["x_first_in"], 16)
            for n in range(SLOTS):
                front(0, n)
            for k in range(K):
                weights(0, 0, k)
            dve.wait_ge(s["x_rest_in"], 16)
            with dve.Fori(0, B - 1) as b:
                batch_steps(b, b + 1)
            batch_steps(B - 1, None)
            with dve.If(is_beyond(dve)):
                general_path()


def kernel(x, L0_conv_W, L0_conv_b, L1_conv_w1, L1_conv_b1, L1_conv_w2, L1_conv_b2, L1_conv_wd):
    import numpy as np
    import concourse.bacc as bacc
    from concourse.bass_utils import run_bass_kernel_spmd

    def taps_first(w):
        w = np.asarray(w)
        return np.ascontiguousarray(w.reshape(w.shape[0], w.shape[1], 9).transpose(1, 2, 0))

    arrays = {
        "x": np.ascontiguousarray(x),
        "W0": np.ascontiguousarray(np.asarray(L0_conv_W).T),
        "b0": np.ascontiguousarray(L0_conv_b),
        "w1": taps_first(L1_conv_w1),
        "b1": np.asarray(L1_conv_b1).reshape(-1, 1),
        "w2": taps_first(L1_conv_w2),
        "b2": np.asarray(L1_conv_b2).reshape(-1, 1),
        "wd": taps_first(L1_conv_wd),
    }
    nc = bacc.Bacc("TRN2", target_bir_lowering=False, num_devices=1)
    args = [nc.dram_tensor(n, a.shape, mybir.dt.from_np(a.dtype), kind="ExternalInput").ap()
            for n, a in arrays.items()]
    out = nc.dram_tensor("out", arrays["x"].shape, F32, kind="ExternalOutput").ap()
    mix_deform_kernel(nc, *args, out)
    r = run_bass_kernel_spmd(nc, [arrays], core_ids=[0])
    return r.results[0]["out"]
```

```python
from contextlib import ExitStack

import concourse.bass as bass
from concourse import mybir

F32 = mybir.dt.float32
F32R = mybir.dt.float32r
I32 = mybir.dt.int32
ACT = mybir.ActivationFunctionType
ALU = mybir.AluOpType
AX = mybir.AxisListType

P = 128


def mix_deform_kernel(nc, x, W0, b0, w1, b1, w2, b2, wd, out):
    B, C, H, WID = x.shape
    NPIX = H * WID
    HALF = NPIX // 2
    G, K = 4, 9
    CG = C // G
    NOFF = 2 * G * K
    REACH = 2
    BLK = 4
    RIM = REACH + 1
    WIN = BLK + 2 * RIM
    CELLS = WIN * WIN
    TOP = 6 * BLK
    BOTTOM_AT = (TOP - WIN) // BLK + 1
    SUP = BLK + 2 * REACH
    ROWT = H // BLK
    NBLK = WID // BLK
    BP = BLK * BLK
    HP = H + 2 * RIM
    CP = H + 2
    QT = NPIX // P
    GN_EPS, NORM_EPS = 1e-5, 1e-8
    BANK = 512
    TURNS = ["tap 0", "tap 1", "tap 2", "windows 0", "tap 3", "tap 4", "tap 5", "windows 1", "tap 6", "tap 7", "tap 8"]
    TGROUPS = len(TURNS)
    WINDOWS_AT = {2: 0, 5: 1}
    VGROUPS = ((0, 3), (3, 6), (6, 8))
    SAMPLED_AT = [hi for _, hi in VGROUPS]
    SLOTS = K * ROWT
    assert C == P and BLK * WID == P and G * CG == C and QT == 8 and ROWT == 8

    ctx = ExitStack()
    with ctx:
        def sb(name, shape, dt=F32):
            return ctx.enter_context(nc.sbuf_tensor(name, shape, dt))

        def pb(name, shape, dt=F32):
            return ctx.enter_context(nc.psum_tensor(name, shape, dt))

        def sem(name):
            return ctx.enter_context(nc.semaphore(name))

        ident = sb("ident", [P, P])
        ones = sb("ones", [P, P])
        avg4 = sb("avg4", [P, P])
        avg4b = sb("avg4b", [P, P])
        cell_idx = sb("cell_idx", [P, SUP])
        grid = sb("grid", [P, 2])
        grid_i = sb("grid_i", [P, 4], I32)
        block_col = sb("block_col", [P, 1])
        eps_col = sb("eps_col", [P, 1])
        table_col = sb("table_col", [P, 1])
        w0_sb = sb("w0_sb", [P, C])
        w1_p = sb("w1_p", [P, 2, K * C], F32R)
        w2_p = sb("w2_p", [P, 2, K * NOFF], F32R)
        wd_sb = sb("wd_sb", [P, K * C])
        b0_row = sb("b0_row", [P, C])
        b1_col = sb("b1_col", [P, 1])
        b2_col = sb("b2_col", [NOFF, 1])
        x_all = sb("x_all", [P, B, NPIX])
        pos_all = sb("pos_all", [P, B, ROWT, NOFF])
        first_bn = sb("first_bn", [P, B, 2, 6])
        first_mv = sb("first_mv", [P, B, 2])
        first_dev = sb("first_dev", [P, B])
        first_varp = sb("first_varp", [P, B])
        first_sd = sb("first_sd", [P, B])
        first_norm = sb("first_norm", [P, 2, B])
        bn = sb("bn", [P, 2, 6])
        mv = sb("mv", [P, 2])
        dev = sb("dev", [P, 1])
        varp = sb("varp", [P, 1])
        mean = sb("mean", [P, 1])
        sd = sb("sd", [P, 1])
        rstd = sb("rstd", [P, 1])
        scratch = sb("scratch", [P, NPIX])
        off_ch = scratch[0:NOFF, :]
        inv2 = sb("inv2", [P, QT])
        floor2 = sb("floor2", [P, QT])
        norm2 = sb("norm2", [P, QT])
        diagonal = sb("diagonal", [P, P])
        inv2_all = sb("inv2_all", [P, NPIX])
        g_sb = inv2_all
        gxT_sum = inv2_all[:, :].rearrange("p (i c) -> p i c", c=C)
        gxT = scratch[:, :].rearrange("p (i c) -> p i c", c=C)
        g_p = sb("g_p", [P, 2, NPIX], F32R)
        rel = sb("rel", [P, 2, HALF])
        inv2_diag = rel[:, :, :].rearrange("p j (i q) -> p (j i) q", q=P)
        sim = sb("sim", [P, 2, NPIX])
        hpad = sb("hpad", [P, HP, HP])
        hpad_p = sb("hpad_p", [P, 2, CP, CP], F32R)
        cpad_p = sb("cpad_p", [P, 2, CP, CP], F32R)
        hcol = sb("hcol", [P, NBLK, HP, WIN])
        tent = sb("tent", [P, NOFF, SUP])
        wpix = sb("wpix", [P, K, G, CELLS])
        wcell = sb("wcell", [CELLS, 2, K, G, P])
        hwin = sb("hwin", [CELLS, 2, NBLK, C])
        val = sb("val", [P, 4, NBLK * K * BP])
        raw = wpix[:, :, :, :].rearrange("p k g q -> p (k g q)")
        w_raw, at = [], 0
        for n in (K * C, K * NOFF):
            w_raw.append(raw[:, at:at + n])
            at += n
        w_parts = [w1_p, w2_p]

        extremes = sb("extremes", [NOFF, 2, B])
        ends = sb("ends", [NOFF, 2])
        farthest = sb("farthest", [NOFF, 1])
        far_all = sb("far_all", [1, 1])
        beyond = sb("beyond", [1, 1], I32)
        norm2nd = sb("norm2nd", [P, B, 2])
        cell32 = sb("cell32", [P, WID])
        tap_at = sb("tap_at", [P, K, 2])
        row_at = sb("row_at", [P, ROWT])
        stat_cur = sb("stat_cur", [P, 3])
        GK = G * K
        place = tent[:, 0:NOFF // SUP, :].rearrange("p a b -> p (a b)")
        tent_y, tent_x, wide_tmp = (raw[:, i * GK * WID:(i + 1) * GK * WID].rearrange("p (n r) -> p n r", r=WID)
                                    for i in range(3))
        strips_flat = hcol[:, :, :, :].rearrange("p u r c -> p (u r c)")
        plane = strips_flat[:, 0:G * P]
        plane_t = strips_flat[:, G * P:2 * G * P]
        h_cur = strips_flat[:, 2 * G * P:2 * G * P + C]
        acc = strips_flat[:, 2 * G * P + C:2 * G * P + C + K * P]
        orelu = sb("orelu", [P, 2, HALF // 2])
        yout = sb("yout", [P, 2, HALF // 2])

        psT = pb("psT", [P, 2, BANK])
        psV = pb("psV", [P, 2, BANK])
        psA = pb("psA", [P, 2, BANK])
        psB = pb("psB", [P, 2, BANK])

        s = {n: sem(n) for n in (
            "x_first_in x_rest_in mix_weights_in conv_weights_in zeroed const_ready rims_zeroed "
            "first_stats first_moments first_mean first_dev first_varp first_var first_sd first_done first_picked "
            "stats_done moments mean_done dev_done varp_done var_done sd_done rstd_done "
            "w_hi_done w_lo_done g_hi_done g_lo_done h_hi_done h_lo_done conv1_hi "
            "g_done diagonal_done norm2_done floor_done inv2_done diag_done spread2_done inv2_all_done scaled_done "
            "gx_done gx_sum_done gxT_done simps_done rel_done sim_done mix_done x1_done h_done "
            "conv1_done cpad_done conv2_done off_done offT_done pos_done "
            "extremes_done ends_done farthest_done far_turned far_all_done flag_done coords_ready "
            "stat2_done g_stat g_h g_hT g_hTs g_place g_shift g_d1 g_f1 g_tent g_zero g_cur g_plane g_turn g_planeT "
            "g_sample g_acc g_conv g_relu g_out g_stored "
            "strips_top strips_bottom dist_done fold_done tent_done weights_done turned turn_free "
            "sampled val_free dconv_done orelu_done yout_done settled grid_ready out_first out_second").split()}
        out_sems = [s["out_first"], s["out_second"]]

        block = ctx.enter_context(nc.Block())

        def batch(ap, b):
            return ap[:, bass.ds(b, 1), :].rearrange("p b n -> p (b n)")

        NORM1, GX = 0, 4
        SCORE = [6 + 3 * i for i in range(QT)]
        SCALE = [8 + 3 * i for i in range(QT)]
        MIX = [10 + 3 * i for i in range(QT)]
        SPREAD2 = 32
        STATS, MEAN, VAR, NORM = 33, 38, 40, 41
        CONV1, CONV2, TURN_OFF = 45, 57, 69
        REST = 3
        DCONV = {0: (range(35, 35 + K), 1, 1), 1: (range(54, 57), 3, 1), 2: (range(SLOTS, SLOTS + 3), 3, 0)}
        DCONV_BANK = {q: (DCONV[q][2] if q in DCONV else 1) for q in range(4)}

        TURNED0, SAMPLED0, DCONV0 = 1, 4, 1
        RIMS = 3
        ZEROED = 6

        def settle(eng):
            eng.sem_inc(s["settled"], 1)

        def is_beyond(eng):
            eng.wait_ge(s["flag_done"], 1)
            return eng.value_load(beyond[0:1, 0:1], min_val=0, max_val=1) > 0

        def part(x, i):
            return x[:, i].bitcast(F32)

        @block.sync
        def _(sp):
            sp.dma_start(x_all[:, 0, :], x[0].rearrange("c h w -> c (h w)")).then_inc(s["x_first_in"], 16)
            sp.dma_start(w0_sb[:, :], W0).then_inc(s["mix_weights_in"], 16)
            sp.dma_start(b0_row[:, :], b0.partition_broadcast(P)).then_inc(s["mix_weights_in"], 16)
            sp.dma_start(b1_col[:, :], b1).then_inc(s["conv_weights_in"], 16)
            sp.dma_start(b2_col[:, :], b2).then_inc(s["conv_weights_in"], 16)
            for dst, src in zip(w_raw + [wd_sb[:, :]], (w1, w2, wd)):
                sp.dma_start(dst, src.rearrange("c k o -> c (k o)")).then_inc(s["conv_weights_in"], 16)
            sp.dma_start(x_all[:, 1:B, :], x[1:B].rearrange("b c h w -> c b (h w)")).then_inc(s["x_rest_in"], 16)
            for half in range(2):
                sp.nop().then_inc(out_sems[half], 16)
            sp.nop().then_inc(s["g_stored"], 16)
            with sp.Fori(0, B) as b:
                for q in range(4):
                    sp.wait_ge(s["yout_done"], 4 * b + q + 1)
                    sp.dma_start(out[bass.ds(b, 1), :, 2 * BLK * q:2 * BLK * (q + 1), :].rearrange("b c h w -> c (b h w)"),
                                 yout[:, q % 2, :]).then_inc(out_sems[q % 2], 16)
            for half in range(2):
                sp.wait_ge(out_sems[half], 16 * (2 * B + 1))
            with sp.If(is_beyond(sp)):
                with sp.Fori(0, B) as b:
                    with sp.Fori(0, ROWT) as t:
                        sp.wait_ge(s["g_out"], ROWT * b + t + 1)
                        sp.dma_start(out[bass.ds(b, 1), :, bass.ds(BLK * t, BLK), :].rearrange("b c h w -> c (b h w)"),
                                     yout[:, 0, 0:P]).then_inc(s["g_stored"], 16)
                sp.wait_ge(s["g_stored"], 16 * (B * ROWT + 1))

        @block.gpsimd
        def _(pool):
            pool.memset(avg4[:, :], 1.0 / 4).then_inc(s["zeroed"], 1)
            pool.memset(eps_col[:, :], GN_EPS).then_inc(s["zeroed"], 1)
            pool.iota(grid_i[:, 0:1], [[0, 1]], base=0, channel_multiplier=1).then_inc(s["zeroed"], 1)
            pool.memset(ident[:, :], 0.0).then_inc(s["zeroed"], 1)
            pool.memset(ones[:, :], 1.0).then_inc(s["zeroed"], 1)
            pool.iota(cell_idx[:, :], [[1, SUP]], base=0, channel_multiplier=0,
                      allow_small_or_imprecise_dtypes=True).then_inc(s["zeroed"], 1)
            pool.wait_ge(s["zeroed"], ZEROED)
            pool.affine_select(out=ident[:, :], in_=ident[:, :], compare_op=ALU.not_equal, fill=1.0,
                               base=0, pattern=[[-1, P]], channel_multiplier=1).then_inc(s["const_ready"], 1)
            a4 = avg4[:, :].rearrange("p (j r) -> p j r", r=4)
            a4b = avg4b[:, :].rearrange("p (j r) -> p j r", r=4)
            pool.affine_select(out=a4b, in_=a4, compare_op=ALU.is_ge, fill=0.0, base=0,
                               pattern=[[-4, P // 4], [0, 4]], channel_multiplier=1).then_inc(s["const_ready"], 1)
            pool.wait_ge(s["const_ready"], 2)
            pool.affine_select(out=a4, in_=a4b, compare_op=ALU.is_ge, fill=0.0, base=3,
                               pattern=[[4, P // 4], [0, 4]], channel_multiplier=-1).then_inc(s["const_ready"], 1)

            pool.memset(hpad_p[:, :, :, :].bitcast(F32), 0.0).then_inc(s["rims_zeroed"], 1)
            pool.memset(cpad_p[:, :, :, :].bitcast(F32), 0.0).then_inc(s["rims_zeroed"], 1)
            pool.memset(hpad[:, :, :], 0.0).then_inc(s["rims_zeroed"], 1)
            pool.wait_ge(s["conv_weights_in"], 5 * 16)
            for w, w_p in zip(w_raw, w_parts):
                pool.tensor_copy(w_p[:, 0], w).then_inc(s["w_hi_done"], 1)
            pool.iota(cell32[:, :], [[1, WID]], base=0, channel_multiplier=0,
                      allow_small_or_imprecise_dtypes=True).then_inc(s["coords_ready"], 1)
            pool.iota(row_at[:, :], [[BLK, ROWT]], base=0, channel_multiplier=0,
                      allow_small_or_imprecise_dtypes=True).then_inc(s["coords_ready"], 1)
            for a, pattern in enumerate(([[1, 3], [0, 3]], [[0, 3], [1, 3]])):
                pool.iota(tap_at[:, :, a:a + 1].rearrange("p (y x) o -> p y (x o)", y=3), pattern, base=-RIM,
                          channel_multiplier=0, allow_small_or_imprecise_dtypes=True).then_inc(s["coords_ready"], 1)

            def front(b):
                for i in range(QT):
                    for j in range(2):
                        pool.wait_ge(s["rel_done"], 2 * (QT * b + i) + j + 1)
                        if j == 0 and i >= 2:
                            pool.wait_ge(s["mix_done"], QT * b + i - 1)
                        pool.tensor_tensor(sim[:, i % 2, j * HALF:(j + 1) * HALF], rel[:, j, :], rel[:, j, :], ALU.mult)\
                            .then_inc(s["sim_done"], 1)

            def strips(b, rows, done):
                for u in range(NBLK):
                    pool.tensor_copy(hcol[:, u, rows, :], hpad[:, rows, BLK * u:BLK * u + WIN]).then_inc(done, 1)

            top, bottom = slice(0, TOP), slice(TOP, HP)

            front(0)
            pool.wait_ge(s["w_lo_done"], len(w_parts))
            pool.memset(wpix[:, :, :, :], 0.0).then_inc(s["rims_zeroed"], 1)
            pool.wait_ge(s["h_done"], 1)
            strips(0, top, s["strips_top"])
            strips(0, bottom, s["strips_bottom"])
            with pool.Fori(0, B - 1) as b:
                front(b + 1)
                pool.wait_ge(s["h_done"], b + 2)
                for t, rows, done in ((TOP // BLK - 1, top, "strips_top"), (ROWT - 1, bottom, "strips_bottom")):
                    pool.wait_ge(s["turned"], (ROWT * b + t) * TGROUPS + TURNS.index("windows 1") + 1 + TURNED0)
                    settle(pool)
                    strips(b + 1, rows, s[done])

        @block.tensor
        def _(pe):
            def product(dst, left, right, start, stop):
                for i, (l, r) in enumerate(((1, 0), (0, 1), (0, 0))):
                    last = pe.matmul(dst, left[l], right[r], start=start and i == 0, stop=stop and i == 2)
                return last

            def parts(x, *index):
                return [x[(slice(None), i) + index] for i in range(2)]

            def first_mean(lo, hi, step):
                if step == 0:
                    pe.wait_ge(s["first_moments"], hi)
                    src, done = first_mv[:, lo:hi, 0:1].rearrange("p b i -> p (b i)"), "first_mean"
                else:
                    pe.wait_ge(s["first_varp"], hi)
                    src, done = first_varp[:, lo:hi], "first_var"
                pe.matmul(psT[:, 0, B * step + lo:B * step + hi], avg4[:, :], src, start=True, stop=True)\
                    .then_inc(s[done], hi - lo)

            def group_mean(b, col):
                if col == 0:
                    pe.wait_ge(s["moments"], b + 1)
                    src = mv[:, 0:1]
                else:
                    pe.wait_ge(s["varp_done"], b + 1)
                    src = varp[:, :]
                pe.matmul(psB[:, 0, col:col + 1], avg4[:, :], src, start=True, stop=True)\
                    .then_inc(s["mean_done" if col == 0 else "var_done"], 1)

            def gx(b):
                pe.wait_ge(s["g_done"], b + 1)
                for i in range(QT):
                    last = pe.matmul(psA[:, i // 4, (i % 4) * C:(i % 4 + 1) * C],
                                     g_sb[:, i * P:(i + 1) * P], w0_sb[:, :], start=True, stop=True)
                last.then_inc(s["gx_done"], 1)



            def spread_norm2(b):
                pe.wait_ge(s["diag_done"], b + 1)
                for i in range(QT):
                    last = pe.matmul(psB[:, i // 4, (i % 4) * P:(i % 4 + 1) * P], ones[:, :], inv2_diag[:, i, :],
                                     start=True, stop=True)
                last.then_inc(s["spread2_done"], 1)

            def score(b, i):
                for j in range(2):
                    if i >= 1:
                        pe.wait_ge(s["rel_done"], 2 * QT * b + 2 * (i - 1) + j + 1)
                    product(psB[:, j, :], parts(g_p, slice(i * P, (i + 1) * P)),
                            parts(g_p, slice(j * HALF, (j + 1) * HALF)), True, True).then_inc(s["simps_done"], 1)

            def mix(b, i):
                pe.wait_ge(s["gxT_done"], QT * b + i + 1)
                for j in range(2):
                    pe.wait_ge(s["sim_done"], 2 * (QT * b + i) + j + 1)
                    last = pe.matmul(psA[:, j, :], gxT[:, i, :], sim[:, i % 2, j * HALF:(j + 1) * HALF],
                                     start=i == 0, stop=i == QT - 1)
                last.then_inc(s["mix_done"], 1)

            def conv(out_of, pad_p, w_p, width, step, done):
                for m in (2 * step, 2 * step + 1):
                    j, k = divmod(m, K)
                    ky, kx = divmod(k, 3)
                    r = ky + j * H // 2
                    last = product(out_of(j), parts(w_p, slice(k * width, (k + 1) * width)),
                                   parts(pad_p, slice(r, r + H // 2), slice(kx, kx + WID)), k == 0, k == K - 1)
                    if k == K - 1:
                        last.then_inc(done, 1)

            def conv1(b, step):
                if step == 0:
                    pe.wait_ge(s["h_lo_done"], b + 1)
                conv(lambda j: psA[:, j, :], hpad_p, w1_p, C, step, s["conv1_done"])

            def conv2(b, step):
                if step == 0:
                    pe.wait_ge(s["cpad_done"], 2 * b + 2)
                    if not isinstance(b, int):
                        pe.wait_ge(s["orelu_done"], 4 * (b - 1) + 2)
                conv(lambda j: psB[0:NOFF, j, :], cpad_p, w2_p, NOFF, step, s["conv2_done"])

            def turn_offsets(b):
                pe.wait_ge(s["off_done"], 2 * b + 2)
                for t in range(ROWT):
                    last = pe.transpose(psA[:, t // 4, (t % 4) * NOFF:(t % 4 + 1) * NOFF],
                                        off_ch[:, t * P:(t + 1) * P], ident[0:NOFF, 0:NOFF])
                last.then_inc(s["offT_done"], 1)

            def front(b, n):
                if n == SCORE[0]:
                    pe.wait_ge(s["g_lo_done"], b + 1)
                if n in SCORE:
                    score(b, SCORE.index(n))
                if n == GX:
                    if isinstance(b, int):
                        pe.wait_ge(s["mix_weights_in"], 2 * 16)
                    gx(b)
                if n in MIX:
                    mix(b, MIX.index(n))
                if n == SPREAD2:
                    spread_norm2(b)
                if n == MEAN:
                    group_mean(b, 0)
                if n == VAR:
                    group_mean(b, 1)
                if n == CONV1 and isinstance(b, int):
                    pe.wait_ge(s["w_lo_done"], len(w_parts))
                if CONV1 <= n < CONV1 + K:
                    conv1(b, n - CONV1)
                if CONV2 <= n < CONV2 + K:
                    conv2(b, n - CONV2)
                if n == TURN_OFF:
                    turn_offsets(b)

            def turns(b, t, what):
                n = TGROUPS * t + TURNS.index(what)
                pe.wait_ge(s["turn_free"], TGROUPS * ROWT * b + n + 1)
                return psT[:, n % 2, :]

            def cut_windows(b, t, part):
                bank = turns(b, t, f"windows {part}")
                for v in range(4):
                    u = 4 * part + v
                    for first, done in ((0, "strips_top"), (BOTTOM_AT, "strips_bottom")):
                        if t == first:
                            pe.wait_ge(s[done], NBLK * b + u + 1)
                    strip = hcol[:, u, BLK * t:BLK * t + WIN, :].rearrange("p r c -> p (r c)")
                    last = pe.transpose(bank[0:CELLS, v * C:(v + 1) * C], strip, ident[:, :])
                last.then_inc(s["turned"], 1)

            def turn_weights(b, t, k):
                pe.wait_ge(s["weights_done"], K * ROWT * b + K * t + k + 1)
                bank = turns(b, t, f"tap {k}")
                for g in range(G):
                    last = pe.transpose(bank[0:CELLS, g * P:(g + 1) * P], wpix[:, k, g, :], ident[:, :])
                last.then_inc(s["turned"], 1)
                if k in WINDOWS_AT:
                    cut_windows(b, t, WINDOWS_AT[k])

            def sample(b, t, u):
                v = [i for i, (lo, hi) in enumerate(VGROUPS) if lo <= u < hi][0]
                n = len(VGROUPS) * t + v
                lo, hi = VGROUPS[v]
                if u == 0:
                    pe.wait_ge(s["turn_free"], TGROUPS * ROWT * b + TGROUPS * (t + 1) + 2)
                if u == lo:
                    pe.wait_ge(s["val_free"], len(VGROUPS) * ROWT * b + n + 1)
                for g in range(G):
                    w = wcell[:, t % 2, :, g, :].rearrange("q k (i c) -> q k i c", i=BLK)
                    last = pe.matmul(psV[g * CG:(g + 1) * CG, n % 2, (u - lo) * K * BP:(u - lo + 1) * K * BP],
                                     hwin[:, t % 2, u, g * CG:(g + 1) * CG],
                                     w[:, :, :, BLK * u:BLK * (u + 1)], start=True, stop=True)
                if u == hi - 1:
                    last.then_inc(s["sampled"], 1)

            def dconv(b, q, nxt, taps):
                bank = psB[:, DCONV_BANK[q], 0:2 * P]
                if 0 in taps:
                    if q == 0 and nxt is not None:
                        pe.wait_ge(s["inv2_all_done"], nxt + 1)
                    pe.wait_ge(s["val_free"], len(VGROUPS) * (ROWT * b + 2 * (q + 1)) + 2)
                v = val[:, 2 * (q % 2):2 * (q % 2) + 2, :].rearrange("p t (u n) -> p (t u) n", u=NBLK)
                for k in taps:
                    last = pe.matmul(bank, wd_sb[:, k * C:(k + 1) * C], v[:, :, k * BP:(k + 1) * BP],
                                     start=k == 0, stop=k == K - 1)
                if K - 1 in taps:
                    last.then_inc(s["dconv_done"], 1)

            def turn_farthest():
                pe.wait_ge(s["farthest_done"], 1)
                pe.transpose(psA[0:1, 0, 0:NOFF], farthest[:, :], ident[0:NOFF, 0:NOFF]).then_inc(s["far_turned"], 1)

            def general_path():
                with pe.Fori(0, B) as b:
                    pe.wait_ge(s["g_h"], b + 1)
                    for i in range(QT):
                        last = pe.transpose(psT[:, i // 4, (i % 4) * C:(i % 4 + 1) * C],
                                            g_sb[:, i * P:(i + 1) * P], ident[:, :])
                    last.then_inc(s["g_hT"], 1)
                    with pe.Fori(0, ROWT) as t:
                        with pe.Fori(0, QT) as m:
                            for k in range(K):
                                n = K * (QT * (ROWT * b + t) + m) + k
                                pe.wait_ge(s["g_plane"], n + 1)
                                for g in range(G):
                                    last = pe.transpose(psA[:, 0, g * P:(g + 1) * P],
                                                        plane[:, g * P:(g + 1) * P], ident[:, :])
                                last.then_inc(s["g_turn"], 1)
                                pe.wait_ge(s["g_planeT"], n + 1)
                                for g in range(G):
                                    last = pe.matmul(psV[g * CG:(g + 1) * CG, 0, 0:P], h_cur[:, g * CG:(g + 1) * CG],
                                                     plane_t[:, g * P:(g + 1) * P], start=True, stop=True)
                                last.then_inc(s["g_sample"], 1)
                        pe.wait_ge(s["g_acc"], K * QT * (ROWT * b + t + 1))
                        for k in range(K):
                            last = pe.matmul(psB[:, 1, 0:P], wd_sb[:, k * C:(k + 1) * C], acc[:, k * P:(k + 1) * P],
                                             start=k == 0, stop=k == K - 1)
                        last.then_inc(s["g_conv"], 1)

            def batch_steps(b, nxt):
                if nxt is None:
                    turn_farthest()
                for t in range(ROWT + 1):
                    for k in range(K):
                        n = K * t + k
                        if t < ROWT:
                            turn_weights(b, t, k)
                        if t >= 1 and k >= 1:
                            sample(b, t - 1, k - 1)
                        for q in range(3):
                            if n in DCONV[q][0]:
                                width = DCONV[q][1]
                                first = width * DCONV[q][0].index(n)
                                dconv(b, q, nxt, range(first, first + width))
                        if nxt is not None:
                            front(nxt, n)
                dconv(b, 3, nxt, range(K))

            pe.nop().then_inc(s["turned"], TURNED0)
            pe.nop().then_inc(s["g_sample"], 1)
            pe.nop().then_inc(s["sampled"], SAMPLED0)
            pe.nop().then_inc(s["dconv_done"], DCONV0)
            pe.wait_ge(s["const_ready"], 3)
            pe.wait_ge(s["zeroed"], ZEROED)
            for step in range(2):
                first_mean(0, 1, step)
            for n in range(SLOTS):
                front(0, n)
                if n in (SCORE[REST + 2], SCORE[REST + 3]):
                    first_mean(1, B, int(n == SCORE[REST + 3]))
            with pe.Fori(0, B - 1) as b:
                batch_steps(b, b + 1)
            batch_steps(B - 1, None)
            with pe.If(is_beyond(pe)):
                general_path()

        @block.scalar
        def _(act):
            def first_std(lo, hi):
                act.wait_ge(s["first_var"], hi)
                act.activation(first_sd[:, lo:hi], psT[:, 0, B + lo:B + hi], ACT.Sqrt, bias=eps_col[:, :])\
                    .then_inc(s["first_sd"], hi - lo)

            def std(b):
                act.wait_ge(s["var_done"], b + 1)
                act.activation(sd[:, :], psB[:, 0, 1:2], ACT.Sqrt, bias=eps_col[:, :]).then_inc(s["sd_done"], 1)

            def front(b, n):
                if n == NORM1 + 2:
                    act.wait_ge(s["g_done"], b + 1)
                    act.activation(g_p[:, 0], g_sb[:, :], ACT.Copy).then_inc(s["g_hi_done"], 1)
                if n in SCORE:
                    i = SCORE.index(n)
                    for j in range(2):
                        act.wait_ge(s["simps_done"], 2 * (QT * b + i) + j + 1)
                        if i >= 1:
                            if j == (i - 1) // (QT // 2):
                                act.wait_ge(s["diagonal_done"], QT * b + i)
                            act.wait_ge(s["sim_done"], 2 * (QT * b + i - 1) + j + 1)
                        act.activation(rel[:, j, :], psB[:, j, :], ACT.Relu).then_inc(s["rel_done"], 1)
                if n == SPREAD2:
                    act.wait_ge(s["spread2_done"], b + 1)
                    act.activation(inv2_all[:, :], psB[:, :, :].rearrange("p j n -> p (j n)"), ACT.Copy)\
                        .then_inc(s["inv2_all_done"], 1)
                if n == VAR:
                    std(b)
                if n == NORM:
                    if isinstance(b, int):
                        act.wait_ge(s["rims_zeroed"], RIMS)
                    act.wait_ge(s["h_done"], b + 1)
                    act.activation(hpad_p[:, 0, 1:1 + H, 1:1 + WID], hpad[:, RIM:RIM + H, RIM:RIM + WID], ACT.Copy)\
                        .then_inc(s["h_hi_done"], 1)
                for j in range(2):
                    if n == CONV1 + K * (j + 1) // 2:
                        if isinstance(b, int):
                            act.wait_ge(s["conv_weights_in"], 5 * 16)
                        act.wait_ge(s["conv1_done"], 2 * b + j + 1)
                        act.activation(cpad_p[:, 0, 1 + j * H // 2:1 + (j + 1) * H // 2, 1:1 + WID],
                                       psA[:, j, :].rearrange("p (h w) -> p h w", w=WID),
                                       ACT.Identity, bias=b1_col[:, :]).then_inc(s["conv1_hi"], 1)
                    if n == CONV2 + K * (j + 1) // 2:
                        act.wait_ge(s["conv2_done"], 2 * b + j + 1)
                        act.activation(off_ch[:, j * HALF:(j + 1) * HALF], psB[0:NOFF, j, :],
                                       ACT.Identity, bias=b2_col[:, :]).then_inc(s["off_done"], 1)

            def evacuate(b, t, what):
                n = TGROUPS * t + TURNS.index(what)
                kind, i = what.split()
                i = int(i)
                if what == TURNS[0]:
                    act.wait_ge(s["sampled"], len(VGROUPS) * (ROWT * b + t - 1) + SAMPLED0)
                act.wait_ge(s["turned"], TGROUPS * ROWT * b + n + 1 + TURNED0)
                if kind == "windows":
                    dst = hwin[:, t % 2, 4 * i:4 * i + 4, :].rearrange("q u c -> q (u c)")
                else:
                    dst = wcell[:, t % 2, i, :, :].rearrange("q g p -> q (g p)")
                act.activation(dst, psT[0:CELLS, n % 2, :], ACT.Copy).then_inc(s["turn_free"], 1)



            def relu_out(b, q):
                act.wait_ge(s["dconv_done"], 4 * b + q + 1 + DCONV0)
                bank = psB[:, DCONV_BANK[q], :]
                for t in range(2):
                    src = bank[:, t * P:(t + 1) * P].rearrange("p (u i j) -> p u i j", u=NBLK, i=BLK)
                    dst = orelu[:, q % 2, t * P:(t + 1) * P].rearrange("p (i u j) -> p u i j", u=NBLK, i=BLK)
                    last = act.activation(dst, src, ACT.Relu)
                last.then_inc(s["orelu_done"], 1)

            def general_path():
                with act.Fori(0, B) as b:
                    act.wait_ge(s["g_hT"], b + 1)
                    act.activation(scratch[:, :],
                                   psT[:, :, :].rearrange("p j n -> p (j n)"), ACT.Copy).then_inc(s["g_hTs"], 1)
                    act.wait_ge(s["g_hTs"], b + 1)
                    settle(act)
                    with act.Fori(0, ROWT) as t:
                        with act.Fori(0, QT) as m:
                            turn = K * (QT * (ROWT * b + t) + m)
                            act.wait_ge(s["g_sample"], turn + 1)
                            settle(act)
                            act.activation(h_cur, gxT[:, bass.ds(m, 1), :].rearrange("p i c -> p (i c)"), ACT.Copy)\
                                .then_inc(s["g_cur"], 1)
                            for k in range(K):
                                act.wait_ge(s["g_turn"], turn + k + 1)
                                act.activation(plane_t, psA[:, 0, :], ACT.Copy).then_inc(s["g_planeT"], 1)
                        act.wait_ge(s["g_conv"], ROWT * b + t + 1)
                        act.activation(orelu[:, 0, 0:P], psB[:, 1, 0:P], ACT.Relu).then_inc(s["g_relu"], 1)

            def batch_steps(b, nxt):
                for t in range(ROWT + 1):
                    for k in range(K):
                        n = K * t + k
                        if t < ROWT:
                            evacuate(b, t, f"tap {k}")
                            if k in WINDOWS_AT:
                                evacuate(b, t, f"windows {WINDOWS_AT[k]}")
                        for q in range(3):
                            if n == DCONV[q][0][-1]:
                                relu_out(b, q)
                        if nxt is not None:
                            front(nxt, n)
                relu_out(b, 3)

            act.nop().then_inc(s["turn_free"], 2)
            act.wait_ge(s["zeroed"], ZEROED)
            act.activation(table_col[:, :], eps_col[:, :], ACT.Sqrt)
            first_std(0, 1)
            for n in range(SLOTS):
                front(0, n)
                if n == SCORE[REST + 3]:
                    first_std(1, B)
            with act.Fori(0, B - 1) as b:
                batch_steps(b, b + 1)
            batch_steps(B - 1, None)
            with act.If(is_beyond(act)):
                general_path()

        @block.vector
        def _(dve):
            def first_moments(lo, hi):
                for b in range(lo, hi):
                    for j in range(2):
                        dve.bn_stats(first_bn[:, b, j, :], x_all[:, b, j * HALF:(j + 1) * HALF])\
                            .then_inc(s["first_stats"], 1)
                for b in range(lo, hi):
                    dve.wait_ge(s["first_stats"], 2 * (b + 1))
                    dve.bn_aggr(first_mv[:, b, :], first_bn[:, b, :, :]).then_inc(s["first_moments"], 1)

            def first_spread(lo, hi):
                n = hi - lo
                dve.wait_ge(s["first_moments"], hi)
                dve.wait_ge(s["first_mean"], hi)
                dve.tensor_copy(first_norm[:, 0, lo:hi], psT[:, 0, lo:hi]).then_inc(s["first_dev"], n)
                dve.tensor_tensor(first_dev[:, lo:hi], first_mv[:, lo:hi, 0:1].rearrange("p b i -> p (b i)"),
                                  psT[:, 0, lo:hi], ALU.subtract).then_inc(s["first_dev"], n)
                dve.wait_ge(s["first_dev"], 3 * lo + 2 * n)
                dve.tensor_tensor(first_varp[:, lo:hi], first_dev[:, lo:hi], first_dev[:, lo:hi], ALU.mult)\
                    .then_inc(s["first_dev"], n)
                dve.wait_ge(s["first_dev"], 3 * hi)
                dve.tensor_tensor(first_varp[:, lo:hi], first_varp[:, lo:hi],
                                  first_mv[:, lo:hi, 1:2].rearrange("p b i -> p (b i)"), ALU.add)\
                    .then_inc(s["first_varp"], n)

            def first_rstd(lo, hi):
                dve.wait_ge(s["first_sd"], hi)
                dve.reciprocal(first_norm[:, 1, lo:hi], first_sd[:, lo:hi]).then_inc(s["first_done"], hi - lo)

            def channel_stats(b):
                settle(dve)
                for j in range(2):
                    dve.bn_stats(bn[:, j, :], batch(x_all, b)[:, j * HALF:(j + 1) * HALF])\
                        .then_inc(s["stats_done"], 1)
                dve.wait_ge(s["stats_done"], 2 * b + 2)
                settle(dve)
                dve.bn_aggr(mv[:, :], bn[:, :, :]).then_inc(s["moments"], 1)

            def spread(b):
                dve.wait_ge(s["moments"], b + 1)
                dve.wait_ge(s["mean_done"], b + 1)
                dve.tensor_copy(mean[:, :], psB[:, 0, 0:1]).then_inc(s["dev_done"], 1)
                dve.tensor_tensor(dev[:, :], mv[:, 0:1], psB[:, 0, 0:1], ALU.subtract).then_inc(s["dev_done"], 1)
                dve.wait_ge(s["dev_done"], 2 * b + 2)
                dve.scalar_tensor_tensor(out=varp[:, :], in0=dev[:, :], scalar=dev[:, :], in1=mv[:, 1:2],
                                         op0=ALU.mult, op1=ALU.add).then_inc(s["varp_done"], 1)

            def normalise_x(b):
                if isinstance(b, int):
                    dve.wait_ge(s["first_done"], b + 1)
                for i, col in enumerate((mean, rstd)):
                    dve.tensor_copy(col[:, :], first_norm[:, i, bass.ds(b, 1)]).then_inc(s["first_picked"], 1)
                dve.wait_ge(s["first_picked"], 2 * b + 2)
                dve.tensor_scalar(g_sb[:, :], batch(x_all, b), mean[:, :], rstd[:, :], ALU.subtract, ALU.mult)\
                    .then_inc(s["g_done"], 1)

            def normalise_x1(b):
                dve.wait_ge(s["sd_done"], b + 1)
                dve.reciprocal(rstd[:, :], sd[:, :]).then_inc(s["rstd_done"], 1)
                dve.wait_ge(s["rstd_done"], b + 1)
                if isinstance(b, int):
                    dve.wait_ge(s["rims_zeroed"], RIMS)
                else:
                    dve.wait_ge(s["strips_bottom"], NBLK * b)
                dve.tensor_scalar(hpad[:, RIM:RIM + H, RIM:RIM + WID], batch(x_all, b).rearrange("p (h w) -> p h w", w=WID),
                                  mean[:, :], rstd[:, :], ALU.subtract, ALU.mult).then_inc(s["h_done"], 1)
                for i, col in enumerate((mean, rstd)):
                    dve.tensor_copy(norm2nd[:, bass.ds(b, 1), i:i + 1].rearrange("p b i -> p (b i)"), col[:, :])\
                        .then_inc(s["stat2_done"], 1)

            def inverse_norm2(b, i):
                m = QT * b + i + 1
                half = i // (QT // 2)
                dve.wait_ge(s["rel_done"], 2 * (m - 1) + half + 1)
                at = i % (QT // 2) * P
                dve.tensor_tensor(diagonal[:, :], rel[:, half, at:at + P], ident[:, :], ALU.mult)\
                    .then_inc(s["diagonal_done"], 1)
                dve.wait_ge(s["diagonal_done"], m)
                dve.tensor_reduce(norm2[:, i:i + 1], diagonal[:, :], AX.X, ALU.add).then_inc(s["norm2_done"], 1)
                dve.wait_ge(s["norm2_done"], m)
                dve.tensor_scalar(floor2[:, i:i + 1], norm2[:, i:i + 1], NORM_EPS ** 2, None, ALU.max)\
                    .then_inc(s["floor_done"], 1)
                dve.wait_ge(s["floor_done"], m)
                dve.reciprocal(inv2[:, i:i + 1], floor2[:, i:i + 1]).then_inc(s["inv2_done"], 1)

            def split_weights():
                for i, (w, w_p) in enumerate(zip(w_raw, w_parts)):
                    dve.wait_ge(s["w_hi_done"], i + 1)
                    dve.tensor_tensor(w_p[:, 1], w, part(w_p, 0), ALU.subtract).then_inc(s["w_lo_done"], 1)

            def add_bias(b):
                dve.wait_ge(s["gx_done"], b + 1)
                dve.wait_ge(s["g_lo_done"], b + 1)
                dve.tensor_tensor(gxT_sum, psA[:, :, :].rearrange("p j (i c) -> p (j i) c", c=C),
                                  b0_row[:, :].unsqueeze(1).to_broadcast([P, QT, C]), ALU.add)\
                    .then_inc(s["gx_sum_done"], 1)

            def scale_gx(b, i):
                dve.wait_ge(s["gx_sum_done"], b + 1)
                dve.wait_ge(s["inv2_done"], QT * b + i + 1)
                dve.tensor_scalar(gxT[:, i, :], gxT_sum[:, i, :], inv2[:, i:i + 1], None, ALU.mult)\
                    .then_inc(s["gxT_done"], 1)



            def split_conv1(b, j):
                dve.wait_ge(s["conv1_hi"], 2 * b + j + 1)
                rows = slice(1 + j * H // 2, 1 + (j + 1) * H // 2)
                dve.scalar_tensor_tensor(out=cpad_p[:, 1, rows, 1:1 + WID],
                                         in0=psA[:, j, :].rearrange("p (h w) -> p h w", w=WID), scalar=b1_col[:, :],
                                         in1=cpad_p[:, 0, rows, 1:1 + WID].bitcast(F32),
                                         op0=ALU.add, op1=ALU.subtract).then_inc(s["cpad_done"], 1)

            def add_mixed(b):
                dve.wait_ge(s["mix_done"], QT * (b + 1))
                dve.wait_ge(s["inv2_all_done"], b + 1)
                dve.tensor_tensor(scratch[:, :], psA[:, :, :].rearrange("p j n -> p (j n)"), inv2_all[:, :], ALU.mult)\
                    .then_inc(s["scaled_done"], 1)
                dve.wait_ge(s["scaled_done"], b + 1)
                xb = batch(x_all, b)
                dve.tensor_tensor(xb, xb, scratch[:, :], ALU.add).then_inc(s["x1_done"], 1)
                dve.wait_ge(s["x1_done"], b + 1)

            def front(b, n):
                if n == NORM1 + 2:
                    dve.wait_ge(s["g_hi_done"], b + 1)
                    dve.tensor_tensor(g_p[:, 1], g_sb[:, :], part(g_p, 0), ALU.subtract).then_inc(s["g_lo_done"], 1)
                if n in SCORE:
                    inverse_norm2(b, SCORE.index(n))
                if n == GX:
                    add_bias(b)
                if n in SCALE:
                    scale_gx(b, SCALE.index(n))
                if n == SPREAD2 - 1:
                    dve.wait_ge(s["sim_done"], 2 * QT * (b + 1))
                    dve.tensor_tensor(inv2_diag, ident[:, :].unsqueeze(1).to_broadcast([P, QT, P]),
                                      inv2[:, :].unsqueeze(2).to_broadcast([P, QT, P]), ALU.mult)\
                        .then_inc(s["diag_done"], 1)
                if n == STATS:
                    add_mixed(b)
                    channel_stats(b)
                if n == MEAN:
                    spread(b)
                if n == NORM:
                    normalise_x1(b)
                    dve.wait_ge(s["h_hi_done"], b + 1)
                    dve.tensor_tensor(hpad_p[:, 1, 1:1 + H, 1:1 + WID], hpad[:, RIM:RIM + H, RIM:RIM + WID],
                                      hpad_p[:, 0, 1:1 + H, 1:1 + WID].bitcast(F32), ALU.subtract)\
                        .then_inc(s["h_lo_done"], 1)
                for j in range(2):
                    if n == CONV1 + K * (j + 1) // 2:
                        split_conv1(b, j)
                if n == TURN_OFF:
                    dve.wait_ge(s["offT_done"], b + 1)
                    for j in range(2):
                        src = psA[:, j, 0:4 * NOFF].rearrange("p (n a) -> p n a", a=2)
                        dst = pos_all[:, bass.ds(b, 1), 4 * j:4 * j + 4, :].rearrange("p b t (n a) -> p (b t n) a", a=2)
                        dve.tensor_tensor(dst, src, grid[:, :].unsqueeze(1).to_broadcast([P, 4 * NOFF // 2, 2]),
                                          ALU.add).then_inc(s["pos_done"], 1)
                if n == TURN_OFF - 1:
                    dve.wait_ge(s["off_done"], 2 * b + 2)
                    for i, op in enumerate((ALU.max, ALU.min)):
                        dve.tensor_reduce(extremes[:, i, bass.ds(b, 1)], off_ch, AX.X, op)\
                            .then_inc(s["extremes_done"], 1)

            def tents(b, t):
                n = ROWT * b + t
                if t == 0:
                    dve.wait_ge(s["pos_done"], 2 * b + 2)
                if not (isinstance(b, int) and n == 0):
                    dve.wait_ge(s["weights_done"], K * n)
                p = pos_all[:, bass.ds(b, 1), t, :].rearrange("p b n -> p (b n)")
                dve.tensor_tensor(tent[:, :, :], p.unsqueeze(2).to_broadcast([P, NOFF, SUP]),
                                  cell_idx[:, :].unsqueeze(1).to_broadcast([P, NOFF, SUP]),
                                  ALU.subtract).then_inc(s["dist_done"], 1)
                dve.wait_ge(s["dist_done"], n + 1)
                dve.scalar_tensor_tensor(out=tent[:, :, :], in0=tent[:, :, :], scalar=-1.0, in1=tent[:, :, :],
                                         op0=ALU.mult, op1=ALU.min).then_inc(s["fold_done"], 1)
                dve.wait_ge(s["fold_done"], n + 1)
                dve.tensor_scalar(tent[:, :, :], tent[:, :, :], 1.0, 0.0, ALU.add, ALU.max)\
                    .then_inc(s["tent_done"], 1)

            def weights(b, t, k):
                if k == 0:
                    tents(b, t)
                    dve.wait_ge(s["tent_done"], ROWT * b + t + 1)
                if not (isinstance(b, int) and ROWT * b + t == 0):
                    dve.wait_ge(s["turned"], TGROUPS * (ROWT * b + t - 1) + TURNS.index(f"tap {k}") + 1 + TURNED0)
                ky, kx = divmod(k, 3)
                tv = tent[:, :, :].rearrange("p (g k a) r -> p g k a r", g=G, a=2)
                ty = tv[:, :, k, 0, :].unsqueeze(3).to_broadcast([P, G, SUP, SUP])
                tx = tv[:, :, k, 1, :].unsqueeze(2).to_broadcast([P, G, SUP, SUP])
                w = wpix[:, k, :, :].rearrange("p g (r c) -> p g r c", c=WIN)
                dve.tensor_tensor(w[:, :, ky:ky + SUP, kx:kx + SUP], ty, tx, ALU.mult)\
                    .then_inc(s["weights_done"], 1)

            def take_samples(b, t, v):
                n = len(VGROUPS) * t + v
                lo, hi = VGROUPS[v]
                dve.wait_ge(s["sampled"], len(VGROUPS) * ROWT * b + n + 1 + SAMPLED0)
                if v == 0 and t % 2 == 0:
                    dve.wait_ge(s["dconv_done"], 4 * b + t // 2 - 1 + DCONV0)
                dve.tensor_copy(val[:, t % 4, lo * K * BP:hi * K * BP], psV[:, n % 2, 0:(hi - lo) * K * BP])\
                    .then_inc(s["val_free"], 1)

            def add_out(b, q):
                dve.wait_ge(s["orelu_done"], 4 * b + q + 1)
                dve.wait_ge(out_sems[q % 2], 16 * (2 * b + q // 2 + 1))
                dve.tensor_tensor(yout[:, q % 2, :], orelu[:, q % 2, :],
                                  batch(x_all, b)[:, q * 2 * P:(q + 1) * 2 * P], ALU.add)\
                    .then_inc(s["yout_done"], 1)

            def find_farthest():
                dve.wait_ge(s["extremes_done"], 2 * B)
                dve.tensor_reduce(ends[:, 0:1], extremes[:, 0, :], AX.X, ALU.max).then_inc(s["ends_done"], 1)
                dve.tensor_reduce(ends[:, 1:2], extremes[:, 1, :], AX.X, ALU.min).then_inc(s["ends_done"], 1)
                dve.wait_ge(s["ends_done"], 2)
                dve.scalar_tensor_tensor(out=farthest[:, :], in0=ends[:, 1:2], scalar=-1.0, in1=ends[:, 0:1],
                                         op0=ALU.mult, op1=ALU.max).then_inc(s["farthest_done"], 1)
                dve.wait_ge(s["far_turned"], 1)
                dve.tensor_reduce(far_all[:, :], psA[0:1, 0, 0:NOFF], AX.X, ALU.max).then_inc(s["far_all_done"], 1)
                dve.wait_ge(s["far_all_done"], 1)
                dve.tensor_scalar(beyond[:, :], far_all[:, :], float(REACH), None, ALU.is_gt)\
                    .then_inc(s["flag_done"], 1)

            def general_tents(b, t):
                n = ROWT * b + t
                pos = pos_all[:, bass.ds(b, 1), bass.ds(t, 1), :].rearrange("p b t n -> p (b t n)")
                dve.tensor_tensor(place.rearrange("p (g k a) -> p g k a", g=G, a=2),
                                  pos.rearrange("p (g k a) -> p g k a", g=G, a=2),
                                  tap_at[:, :, :].unsqueeze(1).to_broadcast([P, G, K, 2]),
                                  ALU.add).then_inc(s["g_place"], 1)
                dve.tensor_copy(stat_cur[:, 2:3], row_at[:, bass.ds(t, 1)]).then_inc(s["g_place"], 1)
                dve.wait_ge(s["g_place"], 2 * n + 2)
                by_axis = place.rearrange("p (n a) -> p n a", a=2)
                rows = by_axis[:, :, 0:1].rearrange("p n o -> p (n o)")
                dve.tensor_scalar(rows, rows, stat_cur[:, 2:3], None, ALU.add).then_inc(s["g_shift"], 1)
                dve.wait_ge(s["g_shift"], n + 1)
                for a, dst in enumerate((tent_y, tent_x)):
                    m = 2 * n + a + 1
                    dve.tensor_tensor(wide_tmp, by_axis[:, :, a:a + 1].to_broadcast([P, GK, WID]),
                                      cell32[:, :].unsqueeze(1).to_broadcast([P, GK, WID]),
                                      ALU.subtract).then_inc(s["g_d1"], 1)
                    dve.wait_ge(s["g_d1"], m)
                    dve.scalar_tensor_tensor(out=dst, in0=wide_tmp, scalar=-1.0, in1=wide_tmp,
                                             op0=ALU.mult, op1=ALU.min).then_inc(s["g_f1"], 1)
                    dve.wait_ge(s["g_f1"], m)
                    dve.tensor_scalar(dst, dst, 1.0, 0.0, ALU.add, ALU.max).then_inc(s["g_tent"], 1)
                dve.memset(acc, 0.0).then_inc(s["g_zero"], 1)
                dve.wait_ge(s["g_tent"], 2 * n + 2)
                dve.wait_ge(s["g_zero"], n + 1)
                settle(dve)

            def general_path():
                dve.wait_ge(out_sems[0], 16 * (2 * B + 1))
                dve.wait_ge(s["stat2_done"], 2 * B)
                with dve.Fori(0, B) as b:
                    dve.tensor_copy(stat_cur[:, 0:2], norm2nd[:, bass.ds(b, 1), :].rearrange("p b i -> p (b i)"))\
                        .then_inc(s["g_stat"], 1)
                    dve.wait_ge(s["g_stat"], b + 1)
                    dve.tensor_scalar(g_sb[:, :], batch(x_all, b), stat_cur[:, 0:1], stat_cur[:, 1:2],
                                      ALU.subtract, ALU.mult).then_inc(s["g_h"], 1)
                    with dve.Fori(0, ROWT) as t:
                        general_tents(b, t)
                        with dve.Fori(0, QT) as m:
                            for k in range(K):
                                n = K * (QT * (ROWT * b + t) + m) + k
                                ty = tent_y.rearrange("p (g k) r -> p g k r", g=G)[:, :, k, bass.ds(BLK * m, BLK)]
                                tx = tent_x.rearrange("p (g k) c -> p g k c", g=G)[:, :, k, :]
                                dve.tensor_tensor(plane.rearrange("p (g r c) -> p g r c", g=G, r=BLK),
                                                  ty.unsqueeze(3).to_broadcast([P, G, BLK, WID]),
                                                  tx.unsqueeze(2).to_broadcast([P, G, BLK, WID]),
                                                  ALU.mult).then_inc(s["g_plane"], 1)
                                dve.wait_ge(s["g_sample"], n + 1 + 1)
                                dve.tensor_tensor(acc[:, k * P:(k + 1) * P], acc[:, k * P:(k + 1) * P], psV[:, 0, 0:P],
                                                  ALU.add)\
                                    .then_inc(s["g_acc"], 1)
                        n = ROWT * b + t
                        dve.wait_ge(s["g_relu"], n + 1)
                        dve.wait_ge(s["g_stored"], 16 * (n + 1))
                        dve.tensor_tensor(yout[:, 0, 0:P], orelu[:, 0, 0:P],
                                          batch(x_all, b)[:, bass.ds(P * t, P)], ALU.add)\
                            .then_inc(s["g_out"], 1)

            def batch_steps(b, nxt):
                if nxt is None:
                    find_farthest()
                for t in range(ROWT + 1):
                    for k in range(K):
                        n = K * t + k
                        if nxt is not None and n == NORM1:
                            normalise_x(nxt)
                        if t < ROWT - 1:
                            weights(b, t + 1, k)
                        if t >= 1 and k in SAMPLED_AT:
                            take_samples(b, t - 1, SAMPLED_AT.index(k))
                        for q in range(3):
                            if n == DCONV[q][0][-1] + 1:
                                add_out(b, q)
                        if nxt is not None:
                            front(nxt, n)
                if nxt is not None:
                    for k in range(K):
                        weights(nxt, 0, k)
                add_out(b, 3)

            dve.nop().then_inc(s["val_free"], 2)
            dve.wait_ge(s["zeroed"], ZEROED)
            dve.tensor_scalar(grid_i[:, 1:2], grid_i[:, 0:1], 5, None, ALU.arith_shift_right)\
                .then_inc(s["grid_ready"], 1)
            dve.tensor_scalar(grid_i[:, 2:3], grid_i[:, 0:1], BLK - 1, None, ALU.bitwise_and)\
                .then_inc(s["grid_ready"], 1)
            dve.wait_ge(s["grid_ready"], 2)
            dve.tensor_scalar(grid[:, :], grid_i[:, 1:3], float(REACH), None, ALU.add).then_inc(s["grid_ready"], 1)
            dve.wait_ge(s["grid_ready"], 3)
            dve.tensor_scalar(grid_i[:, 3:4], grid_i[:, 0:1], WID - BLK, None, ALU.bitwise_and)\
                .then_inc(s["grid_ready"], 1)
            dve.wait_ge(s["grid_ready"], 4)
            dve.tensor_copy(block_col[:, :], grid_i[:, 3:4]).then_inc(s["grid_ready"], 1)
            dve.wait_ge(s["grid_ready"], 5)
            dve.wait_ge(s["x_first_in"], 16)
            first_moments(0, 1)
            first_spread(0, 1)
            first_rstd(0, 1)
            normalise_x(0)
            for n in range(SLOTS):
                front(0, n)
                if n == SCORE[REST] - 1:
                    dve.wait_ge(s["x_rest_in"], 16)
                    first_moments(1, B)
                if n == SCORE[REST + 2]:
                    first_spread(1, B)
                if n == SCORE[REST + 3]:
                    first_rstd(1, B)
                if n == SCORE[REST + 3]:
                    split_weights()
            dve.wait_ge(s["coords_ready"], 4)
            dve.tensor_scalar(tap_at[:, :, 1:2], tap_at[:, :, 1:2], block_col[:, :], None, ALU.add)\
                .then_inc(s["grid_ready"], 1)
            dve.wait_ge(s["rims_zeroed"], RIMS + 1)
            for k in range(K):
                weights(0, 0, k)
            with dve.Fori(0, B - 1) as b:
                batch_steps(b, b + 1)
            batch_steps(B - 1, None)
            with dve.If(is_beyond(dve)):
                general_path()


def kernel(x, L0_conv_W, L0_conv_b, L1_conv_w1, L1_conv_b1, L1_conv_w2, L1_conv_b2, L1_conv_wd):
    import numpy as np
    import concourse.bacc as bacc
    from concourse.bass_utils import run_bass_kernel_spmd

    def taps_first(w):
        w = np.asarray(w)
        return np.ascontiguousarray(w.reshape(w.shape[0], w.shape[1], 9).transpose(1, 2, 0))

    arrays = {
        "x": np.ascontiguousarray(x),
        "W0": np.ascontiguousarray(np.asarray(L0_conv_W).T),
        "b0": np.ascontiguousarray(L0_conv_b),
        "w1": taps_first(L1_conv_w1),
        "b1": np.asarray(L1_conv_b1).reshape(-1, 1),
        "w2": taps_first(L1_conv_w2),
        "b2": np.asarray(L1_conv_b2).reshape(-1, 1),
        "wd": taps_first(L1_conv_wd),
    }
    nc = bacc.Bacc("TRN2", target_bir_lowering=False, num_devices=1)
    args = [nc.dram_tensor(n, a.shape, mybir.dt.from_np(a.dtype), kind="ExternalInput").ap()
            for n, a in arrays.items()]
    out = nc.dram_tensor("out", arrays["x"].shape, F32, kind="ExternalOutput").ap()
    mix_deform_kernel(nc, *args, out)
    r = run_bass_kernel_spmd(nc, [arrays], core_ids=[0])
    return r.results[0]["out"]
```

```python
from contextlib import ExitStack

import concourse.bass as bass
from concourse import mybir

F32 = mybir.dt.float32
F32R = mybir.dt.float32r
I32 = mybir.dt.int32
ACT = mybir.ActivationFunctionType
ALU = mybir.AluOpType
AX = mybir.AxisListType

P = 128


def mix_deform_kernel(nc, x, W0, b0, w1, b1, w2, b2, wd, out):
    B, C, H, WID = x.shape
    NPIX = H * WID
    HALF = NPIX // 2
    G, K = 4, 9
    CG = C // G
    NOFF = 2 * G * K
    REACH = 2
    BLK = 4
    RIM = REACH + 1
    WIN = BLK + 2 * RIM
    CELLS = WIN * WIN
    TOP = 6 * BLK
    BOTTOM_AT = (TOP - WIN) // BLK + 1
    SUP = BLK + 2 * REACH
    ROWT = H // BLK
    NBLK = WID // BLK
    BP = BLK * BLK
    HP = H + 2 * RIM
    CP = H + 2
    V, PAIRS = 4, H // 2
    QT = NPIX // P
    GN_EPS, NORM_EPS = 1e-5, 1e-8
    BANK = 512
    TURNS = ["tap 0", "tap 1", "tap 2", "windows 0", "tap 3", "tap 4", "tap 5", "windows 1", "tap 6", "tap 7", "tap 8"]
    TGROUPS = len(TURNS)
    WINDOWS_AT = {2: 0, 5: 1}
    VGROUPS = ((0, 3), (3, 6), (6, 8))
    SAMPLED_AT = [hi for _, hi in VGROUPS]
    SLOTS = K * ROWT
    assert C == P and BLK * WID == P and G * CG == C and QT == 8 and ROWT == 8

    ctx = ExitStack()
    with ctx:
        def sb(name, shape, dt=F32):
            return ctx.enter_context(nc.sbuf_tensor(name, shape, dt))

        def pb(name, shape, dt=F32):
            return ctx.enter_context(nc.psum_tensor(name, shape, dt))

        def sem(name):
            return ctx.enter_context(nc.semaphore(name))

        ident = sb("ident", [P, P])
        ones = sb("ones", [P, P])
        avg4 = sb("avg4", [P, P])
        avg4b = sb("avg4b", [P, P])
        cell_idx = sb("cell_idx", [P, SUP])
        grid = sb("grid", [P, 2])
        grid_i = sb("grid_i", [P, 4], I32)
        block_col = sb("block_col", [P, 1])
        eps_col = sb("eps_col", [P, 1])
        table_col = sb("table_col", [P, 1])
        w0_sb = sb("w0_sb", [P, C])
        w1_p = sb("w1_p", [P, 2, V * 3 * C], F32R)
        w2_p = sb("w2_p", [P, 2, V * 3 * NOFF], F32R)
        wd_sb = sb("wd_sb", [P, K * C])
        b0_row = sb("b0_row", [P, C])
        b1_col = sb("b1_col", [P, 1])
        b2_col = sb("b2_col", [NOFF, 1])
        x_all = sb("x_all", [P, B, NPIX])
        pos_all = sb("pos_all", [P, B, ROWT, NOFF])
        first_bn = sb("first_bn", [P, B, 2, 6])
        first_mv = sb("first_mv", [P, B, 2])
        first_dev = sb("first_dev", [P, B])
        first_varp = sb("first_varp", [P, B])
        first_sd = sb("first_sd", [P, B])
        first_norm = sb("first_norm", [P, 2, B])
        bn = sb("bn", [P, 2, 6])
        mv = sb("mv", [P, 2])
        dev = sb("dev", [P, 1])
        varp = sb("varp", [P, 1])
        mean = sb("mean", [P, 1])
        sd = sb("sd", [P, 1])
        rstd = sb("rstd", [P, 1])
        scratch = sb("scratch", [P, NPIX])
        off_ch = scratch[0:NOFF, :]
        norm2 = sb("norm2", [P, QT])
        floor2 = sb("floor2", [P, QT])
        inv2 = sb("inv2", [P, QT])
        diagonal = sb("diagonal", [P, P])
        inv2_all = sb("inv2_all", [P, NPIX])
        g_sb = inv2_all
        gxT_sum = inv2_all[:, :].rearrange("p (i c) -> p i c", c=C)
        gxT = scratch[:, :].rearrange("p (i c) -> p i c", c=C)
        g_p = sb("g_p", [P, 2, NPIX], F32R)
        rel = sb("rel", [P, 2, HALF])
        combo = sb("combo", [P, 2, PAIRS, CP])
        inv2_diag = combo[:, :, :, :].rearrange("p e i c -> p (e i c)")[:, 0:NPIX].rearrange("p (i q) -> p i q", q=P)
        sim = sb("sim", [P, 2, NPIX])
        hpad = sb("hpad", [P, HP, HP])
        conv1_pad = sb("conv1_pad", [P, CP, CP])
        combo_p = sb("combo_p", [P, 2, V, PAIRS, CP], F32R)
        m1, m1_plus, m1_minus = rel[:, 0, :], rel[:, 1, :], inv2_all[:, 0:HALF]
        hcol = sb("hcol", [P, NBLK, HP, WIN])
        tent = sb("tent", [P, NOFF, SUP])
        wpix = sb("wpix", [P, K, G, CELLS])
        wcell = sb("wcell", [CELLS, 2, K, G, P])
        hwin = sb("hwin", [CELLS, 2, NBLK, C])
        val = sb("val", [P, 4, NBLK * K * BP])
        raw = wpix[:, :, :, :].rearrange("p k g q -> p (k g q)")
        w_raw, at = [], 0
        for n in (K * C, K * NOFF):
            w_raw.append(raw[:, at:at + n])
            at += n
        w_parts = [w1_p, w2_p]
        w_combos = []
        for w, width in zip(w_raw, (C, NOFF)):
            n = 3 * width
            w_combos.append([w[:, 0:n], raw[:, at:at + n], raw[:, at + n:at + 2 * n], w[:, 2 * n:3 * n]])
            at += 2 * n

        extremes = sb("extremes", [NOFF, 2, B])
        ends = sb("ends", [NOFF, 2])
        farthest = sb("farthest", [NOFF, 1])
        far_all = sb("far_all", [1, 1])
        beyond = sb("beyond", [1, 1], I32)
        norm2nd = sb("norm2nd", [P, B, 2])
        cell32 = sb("cell32", [P, WID])
        tap_at = sb("tap_at", [P, K, 2])
        row_at = sb("row_at", [P, ROWT])
        stat_cur = sb("stat_cur", [P, 3])
        GK = G * K
        place = tent[:, 0:NOFF // SUP, :].rearrange("p a b -> p (a b)")
        tent_y, tent_x, wide_tmp = (raw[:, i * GK * WID:(i + 1) * GK * WID].rearrange("p (n r) -> p n r", r=WID)
                                    for i in range(3))
        strips_flat = hcol[:, :, :, :].rearrange("p u r c -> p (u r c)")
        plane = strips_flat[:, 0:G * P]
        plane_t = strips_flat[:, G * P:2 * G * P]
        h_cur = strips_flat[:, 2 * G * P:2 * G * P + C]
        acc = strips_flat[:, 2 * G * P + C:2 * G * P + C + K * P]
        orelu = sb("orelu", [P, 2, HALF // 2])
        yout = sb("yout", [P, 2, HALF // 2])

        psT = pb("psT", [P, 2, BANK])
        psV = pb("psV", [P, 2, BANK])
        psA = pb("psA", [P, 2, BANK])
        psB = pb("psB", [P, 2, BANK])

        s = {n: sem(n) for n in (
            "x_first_in x_rest_in mix_weights_in conv_weights_in zeroed const_ready rims_zeroed "
            "first_stats first_moments first_mean first_dev first_varp first_var first_sd first_done first_picked "
            "stats_done moments mean_done dev_done varp_done var_done sd_done rstd_done "
            "w_half_sum w_combined w_hi_done w_lo_done g_hi_done g_lo_done combo_done combo_hi combo_lo "
            "g_done diagonal_done norm2_done floor_done inv2_done diag_done spread2_done inv2_all_done scaled_done "
            "gx_done gx_sum_done gxT_done simps_done rel_done sim_done mix_done x1_done h_done "
            "m_done m1_done m1_sums conv1_done off_done offT_done pos_done "
            "extremes_done ends_done farthest_done far_turned far_all_done flag_done coords_ready "
            "stat2_done g_stat g_h g_hT g_hTs g_place g_shift g_d1 g_f1 g_tent g_zero g_cur g_plane g_turn g_planeT "
            "g_sample g_acc g_conv g_relu g_out g_stored "
            "strips_top strips_bottom dist_done fold_done tent_done weights_done turned turn_free "
            "sampled val_free dconv_done orelu_done yout_done settled grid_ready out_first out_second").split()}
        out_sems = [s["out_first"], s["out_second"]]

        block = ctx.enter_context(nc.Block())

        def batch(ap, b):
            return ap[:, bass.ds(b, 1), :].rearrange("p b n -> p (b n)")

        NORM1, GX = 0, 4
        SCORE = [6 + 3 * i for i in range(QT)]
        SCALE = [8 + 3 * i for i in range(QT)]
        MIX = [10 + 3 * i for i in range(QT)]
        SPREAD2 = SCALE[-1] + 1
        STATS, MEAN, VAR, NORM = 32, 37, 39, 40
        COMBINE, CONV = (41, 50), (43, 54)
        TURN_OFF = (62, 63)
        EXTREMES = 65
        REST = (SCORE[5], SCORE[7])
        W_COMBINE, W_HI, W_LO = (SCALE[4], SCALE[5]), (SCORE[5], SCORE[6]), (SCALE[6], SCALE[7])
        DCONV = {0: (range(35, 35 + K), 1, 1), 1: (range(50, 53), 3, 1), 2: (range(SLOTS, SLOTS + 3), 3, 0)}
        DCONV_BANK = {q: (DCONV[q][2] if q in DCONV else 1) for q in range(4)}

        TURNED0, SAMPLED0, DCONV0 = 1, 4, 2
        RIMS = 2
        ZEROED = 6

        def settle(eng):
            eng.sem_inc(s["settled"], 1)

        def by_combo(w_p, i):
            n = w_p.shape[2] // V
            return [w_p[:, i, v * n:(v + 1) * n] for v in range(V)]

        def is_beyond(eng):
            eng.wait_ge(s["flag_done"], 1)
            return eng.value_load(beyond[0:1, 0:1], min_val=0, max_val=1) > 0

        def part(x, i):
            return x[:, i].bitcast(F32)

        @block.sync
        def _(sp):
            sp.dma_start(x_all[:, 0, :], x[0].rearrange("c h w -> c (h w)")).then_inc(s["x_first_in"], 16)
            sp.dma_start(w0_sb[:, :], W0).then_inc(s["mix_weights_in"], 16)
            sp.dma_start(b0_row[:, :], b0.partition_broadcast(P)).then_inc(s["mix_weights_in"], 16)
            sp.dma_start(b1_col[:, :], b1).then_inc(s["conv_weights_in"], 16)
            sp.dma_start(b2_col[:, :], b2).then_inc(s["conv_weights_in"], 16)
            for dst, src in zip(w_raw + [wd_sb[:, :]], (w1, w2, wd)):
                sp.dma_start(dst, src.rearrange("c k o -> c (k o)")).then_inc(s["conv_weights_in"], 16)
            sp.dma_start(x_all[:, 1:B, :], x[1:B].rearrange("b c h w -> c b (h w)")).then_inc(s["x_rest_in"], 16)
            for half in range(2):
                sp.nop().then_inc(out_sems[half], 16)
            sp.nop().then_inc(s["g_stored"], 16)
            with sp.Fori(0, B) as b:
                for q in range(4):
                    sp.wait_ge(s["yout_done"], 4 * b + q + 1)
                    sp.dma_start(out[bass.ds(b, 1), :, 2 * BLK * q:2 * BLK * (q + 1), :].rearrange("b c h w -> c (b h w)"),
                                 yout[:, q % 2, :]).then_inc(out_sems[q % 2], 16)
            for half in range(2):
                sp.wait_ge(out_sems[half], 16 * (2 * B + 1))
            with sp.If(is_beyond(sp)):
                with sp.Fori(0, B) as b:
                    with sp.Fori(0, ROWT) as t:
                        sp.wait_ge(s["g_out"], ROWT * b + t + 1)
                        sp.dma_start(out[bass.ds(b, 1), :, bass.ds(BLK * t, BLK), :].rearrange("b c h w -> c (b h w)"),
                                     yout[:, 0, 0:P]).then_inc(s["g_stored"], 16)
                sp.wait_ge(s["g_stored"], 16 * (B * ROWT + 1))

        @block.gpsimd
        def _(pool):
            pool.memset(avg4[:, :], 1.0 / 4).then_inc(s["zeroed"], 1)
            pool.memset(eps_col[:, :], GN_EPS).then_inc(s["zeroed"], 1)
            pool.iota(grid_i[:, 0:1], [[0, 1]], base=0, channel_multiplier=1).then_inc(s["zeroed"], 1)
            pool.memset(ident[:, :], 0.0).then_inc(s["zeroed"], 1)
            pool.memset(ones[:, :], 1.0).then_inc(s["zeroed"], 1)
            pool.iota(cell_idx[:, :], [[1, SUP]], base=0, channel_multiplier=0,
                      allow_small_or_imprecise_dtypes=True).then_inc(s["zeroed"], 1)
            pool.wait_ge(s["zeroed"], ZEROED)
            pool.affine_select(out=ident[:, :], in_=ident[:, :], compare_op=ALU.not_equal, fill=1.0,
                               base=0, pattern=[[-1, P]], channel_multiplier=1).then_inc(s["const_ready"], 1)
            a4 = avg4[:, :].rearrange("p (j r) -> p j r", r=4)
            a4b = avg4b[:, :].rearrange("p (j r) -> p j r", r=4)
            pool.affine_select(out=a4b, in_=a4, compare_op=ALU.is_ge, fill=0.0, base=0,
                               pattern=[[-4, P // 4], [0, 4]], channel_multiplier=1).then_inc(s["const_ready"], 1)
            pool.wait_ge(s["const_ready"], 2)
            pool.affine_select(out=a4, in_=a4b, compare_op=ALU.is_ge, fill=0.0, base=3,
                               pattern=[[4, P // 4], [0, 4]], channel_multiplier=-1).then_inc(s["const_ready"], 1)

            pool.memset(conv1_pad[:, :, :], 0.0).then_inc(s["rims_zeroed"], 1)
            pool.memset(hpad[:, :, :], 0.0).then_inc(s["rims_zeroed"], 1)
            pool.iota(cell32[:, :], [[1, WID]], base=0, channel_multiplier=0,
                      allow_small_or_imprecise_dtypes=True).then_inc(s["coords_ready"], 1)
            pool.iota(row_at[:, :], [[BLK, ROWT]], base=0, channel_multiplier=0,
                      allow_small_or_imprecise_dtypes=True).then_inc(s["coords_ready"], 1)
            for a, pattern in enumerate(([[1, 3], [0, 3]], [[0, 3], [1, 3]])):
                pool.iota(tap_at[:, :, a:a + 1].rearrange("p (y x) o -> p y (x o)", y=3), pattern, base=-RIM,
                          channel_multiplier=0, allow_small_or_imprecise_dtypes=True).then_inc(s["coords_ready"], 1)

            def front(b):
                for i in range(QT):
                    for j in range(2):
                        pool.wait_ge(s["rel_done"], 2 * (QT * b + i) + j + 1)
                        if j == 0 and i >= 2:
                            pool.wait_ge(s["mix_done"], QT * b + i - 1)
                        pool.tensor_tensor(sim[:, i % 2, j * HALF:(j + 1) * HALF], rel[:, j, :], rel[:, j, :], ALU.mult)\
                            .then_inc(s["sim_done"], 1)

            def strips(b, rows, done):
                for u in range(NBLK):
                    pool.tensor_copy(hcol[:, u, rows, :], hpad[:, rows, BLK * u:BLK * u + WIN]).then_inc(done, 1)

            top, bottom = slice(0, TOP), slice(TOP, HP)

            front(0)
            pool.wait_ge(s["w_lo_done"], V * len(w_parts))
            pool.memset(wpix[:, :, :, :], 0.0).then_inc(s["rims_zeroed"], 1)
            pool.wait_ge(s["h_done"], 1)
            strips(0, top, s["strips_top"])
            strips(0, bottom, s["strips_bottom"])
            with pool.Fori(0, B - 1) as b:
                front(b + 1)
                pool.wait_ge(s["h_done"], b + 2)
                for t, rows, done in ((TOP // BLK - 1, top, "strips_top"), (ROWT - 1, bottom, "strips_bottom")):
                    pool.wait_ge(s["turned"], (ROWT * b + t) * TGROUPS + TURNS.index("windows 1") + 1 + TURNED0)
                    settle(pool)
                    strips(b + 1, rows, s[done])

        @block.tensor
        def _(pe):
            def product(dst, left, right, start, stop):
                for i, (l, r) in enumerate(((1, 0), (0, 1), (0, 0))):
                    last = pe.matmul(dst, left[l], right[r], start=start and i == 0, stop=stop and i == 2)
                return last

            def parts(x, *index):
                return [x[(slice(None), i) + index] for i in range(2)]

            def first_mean(lo, hi, step):
                if step == 0:
                    pe.wait_ge(s["first_moments"], hi)
                    src, done = first_mv[:, lo:hi, 0:1].rearrange("p b i -> p (b i)"), "first_mean"
                else:
                    pe.wait_ge(s["first_varp"], hi)
                    src, done = first_varp[:, lo:hi], "first_var"
                pe.matmul(psT[:, 0, B * step + lo:B * step + hi], avg4[:, :], src, start=True, stop=True)\
                    .then_inc(s[done], hi - lo)

            def group_mean(b, col):
                if col == 0:
                    pe.wait_ge(s["moments"], b + 1)
                    src = mv[:, 0:1]
                else:
                    pe.wait_ge(s["varp_done"], b + 1)
                    src = varp[:, :]
                pe.matmul(psB[:, 0, col:col + 1], avg4[:, :], src, start=True, stop=True)\
                    .then_inc(s["mean_done" if col == 0 else "var_done"], 1)

            def gx(b):
                pe.wait_ge(s["g_done"], b + 1)
                for i in range(QT):
                    last = pe.matmul(psA[:, i // 4, (i % 4) * C:(i % 4 + 1) * C],
                                     g_sb[:, i * P:(i + 1) * P], w0_sb[:, :], start=True, stop=True)
                last.then_inc(s["gx_done"], 1)

            def spread_norm2(b):
                pe.wait_ge(s["diag_done"], b + 1)
                for j in range(2):
                    last = pe.matmul(psB[:, j, :], ones[:, :],
                                     inv2_diag[:, QT // 2 * j:QT // 2 * (j + 1), :].rearrange("p i q -> p (i q)"),
                                     start=True, stop=True)
                last.then_inc(s["spread2_done"], 1)

            def score(b, i):
                for j in range(2):
                    if i >= 1:
                        pe.wait_ge(s["rel_done"], 2 * QT * b + 2 * (i - 1) + j + 1)
                    product(psB[:, j, :], parts(g_p, slice(i * P, (i + 1) * P)),
                            parts(g_p, slice(j * HALF, (j + 1) * HALF)), True, True).then_inc(s["simps_done"], 1)

            def mix(b, i):
                pe.wait_ge(s["gxT_done"], QT * b + i + 1)
                for j in range(2):
                    pe.wait_ge(s["sim_done"], 2 * (QT * b + i) + j + 1)
                    last = pe.matmul(psA[:, j, :], gxT[:, i, :], sim[:, i % 2, j * HALF:(j + 1) * HALF],
                                     start=i == 0, stop=i == QT - 1)
                last.then_inc(s["mix_done"], 1)

            def conv(b, which, w_p, width, step):
                for m in (2 * step, 2 * step + 1):
                    v, kx = divmod(m, 3)
                    n = V * (2 * b + which) + v + 1
                    bank = (psA if v < 2 else psB)[0:width, v % 2, :]
                    if kx == 0:
                        pe.wait_ge(s["combo_lo"], n)
                        if v == V - 1 and not isinstance(b, int):
                            pe.wait_ge(s["orelu_done"], 4 * (b - 1) + which + 1)
                    last = product(bank, parts(w_p, slice(m * width, (m + 1) * width)),
                                   parts(combo_p, v, slice(None), slice(kx, kx + WID)), kx == 0, kx == 2)
                    if kx == 2:
                        last.then_inc(s["m_done"], 1)

            def turn_offsets(b, j):
                pe.wait_ge(s["off_done"], 2 * b + 2)
                for i in range(4):
                    t = 4 * j + i
                    last = pe.transpose(psA[:, j, i * NOFF:(i + 1) * NOFF],
                                        off_ch[:, t * P:(t + 1) * P], ident[0:NOFF, 0:NOFF])
                last.then_inc(s["offT_done"], 1)

            def front(b, n):
                if n == SCORE[0]:
                    pe.wait_ge(s["g_lo_done"], b + 1)
                if n in SCORE:
                    score(b, SCORE.index(n))
                if n == GX:
                    if isinstance(b, int):
                        pe.wait_ge(s["mix_weights_in"], 2 * 16)
                    gx(b)
                if n in MIX:
                    mix(b, MIX.index(n))
                if n == SPREAD2:
                    spread_norm2(b)
                if n == MEAN:
                    group_mean(b, 0)
                if n == VAR:
                    group_mean(b, 1)
                if n == CONV[0] and isinstance(b, int):
                    pe.wait_ge(s["w_lo_done"], V * len(w_parts))
                for which, (w_p, width) in enumerate(((w1_p, C), (w2_p, NOFF))):
                    if 0 <= n - CONV[which] < 3 * V // 2:
                        conv(b, which, w_p, width, n - CONV[which])
                if n in TURN_OFF:
                    turn_offsets(b, TURN_OFF.index(n))

            def turns(b, t, what):
                n = TGROUPS * t + TURNS.index(what)
                pe.wait_ge(s["turn_free"], TGROUPS * ROWT * b + n + 1)
                return psT[:, n % 2, :]

            def cut_windows(b, t, part):
                bank = turns(b, t, f"windows {part}")
                for v in range(4):
                    u = 4 * part + v
                    for first, done in ((0, "strips_top"), (BOTTOM_AT, "strips_bottom")):
                        if t == first:
                            pe.wait_ge(s[done], NBLK * b + u + 1)
                    strip = hcol[:, u, BLK * t:BLK * t + WIN, :].rearrange("p r c -> p (r c)")
                    last = pe.transpose(bank[0:CELLS, v * C:(v + 1) * C], strip, ident[:, :])
                last.then_inc(s["turned"], 1)

            def turn_weights(b, t, k):
                pe.wait_ge(s["weights_done"], K * ROWT * b + K * t + k + 1)
                bank = turns(b, t, f"tap {k}")
                for g in range(G):
                    last = pe.transpose(bank[0:CELLS, g * P:(g + 1) * P], wpix[:, k, g, :], ident[:, :])
                last.then_inc(s["turned"], 1)
                if k in WINDOWS_AT:
                    cut_windows(b, t, WINDOWS_AT[k])

            def sample(b, t, u):
                v = [i for i, (lo, hi) in enumerate(VGROUPS) if lo <= u < hi][0]
                n = len(VGROUPS) * t + v
                lo, hi = VGROUPS[v]
                if u == 0:
                    pe.wait_ge(s["turn_free"], TGROUPS * ROWT * b + TGROUPS * (t + 1) + 2)
                if u == lo:
                    pe.wait_ge(s["val_free"], len(VGROUPS) * ROWT * b + n + 1)
                for g in range(G):
                    w = wcell[:, t % 2, :, g, :].rearrange("q k (i c) -> q k i c", i=BLK)
                    last = pe.matmul(psV[g * CG:(g + 1) * CG, n % 2, (u - lo) * K * BP:(u - lo + 1) * K * BP],
                                     hwin[:, t % 2, u, g * CG:(g + 1) * CG],
                                     w[:, :, :, BLK * u:BLK * (u + 1)], start=True, stop=True)
                if u == hi - 1:
                    last.then_inc(s["sampled"], 1)

            def dconv(b, q, nxt, taps):
                bank = psB[:, DCONV_BANK[q], 0:2 * P]
                if 0 in taps:
                    if q == 0 and nxt is not None:
                        pe.wait_ge(s["inv2_all_done"], nxt + 1)
                    if q == 1 and nxt is not None:
                        pe.wait_ge(s["conv1_done"], 2 * nxt + 2)
                    pe.wait_ge(s["val_free"], len(VGROUPS) * (ROWT * b + 2 * (q + 1)) + 2)
                v = val[:, 2 * (q % 2):2 * (q % 2) + 2, :].rearrange("p t (u n) -> p (t u) n", u=NBLK)
                for k in taps:
                    last = pe.matmul(bank, wd_sb[:, k * C:(k + 1) * C], v[:, :, k * BP:(k + 1) * BP],
                                     start=k == 0, stop=k == K - 1)
                if K - 1 in taps:
                    last.then_inc(s["dconv_done"], 1)

            def turn_farthest():
                pe.wait_ge(s["farthest_done"], 1)
                pe.transpose(psA[0:1, 0, 0:NOFF], farthest[:, :], ident[0:NOFF, 0:NOFF]).then_inc(s["far_turned"], 1)

            def general_path():
                with pe.Fori(0, B) as b:
                    pe.wait_ge(s["g_h"], b + 1)
                    for i in range(QT):
                        last = pe.transpose(psT[:, i // 4, (i % 4) * C:(i % 4 + 1) * C],
                                            g_sb[:, i * P:(i + 1) * P], ident[:, :])
                    last.then_inc(s["g_hT"], 1)
                    with pe.Fori(0, ROWT) as t:
                        with pe.Fori(0, QT) as m:
                            pe.wait_ge(s["g_cur"], QT * (ROWT * b + t) + m + 1)
                            for k in range(K):
                                n = K * (QT * (ROWT * b + t) + m) + k
                                pe.wait_ge(s["g_plane"], n + 1)
                                for g in range(G):
                                    last = pe.transpose(psA[:, 0, g * P:(g + 1) * P],
                                                        plane[:, g * P:(g + 1) * P], ident[:, :])
                                last.then_inc(s["g_turn"], 1)
                                pe.wait_ge(s["g_planeT"], n + 1)
                                for g in range(G):
                                    last = pe.matmul(psV[g * CG:(g + 1) * CG, 0, 0:P], h_cur[:, g * CG:(g + 1) * CG],
                                                     plane_t[:, g * P:(g + 1) * P], start=True, stop=True)
                                last.then_inc(s["g_sample"], 1)
                        pe.wait_ge(s["g_acc"], K * QT * (ROWT * b + t + 1))
                        for k in range(K):
                            last = pe.matmul(psB[:, 1, 0:P], wd_sb[:, k * C:(k + 1) * C], acc[:, k * P:(k + 1) * P],
                                             start=k == 0, stop=k == K - 1)
                        last.then_inc(s["g_conv"], 1)

            def batch_steps(b, nxt):
                if nxt is None:
                    turn_farthest()
                for t in range(ROWT + 1):
                    for k in range(K):
                        n = K * t + k
                        if t < ROWT:
                            turn_weights(b, t, k)
                        if t >= 1 and k >= 1:
                            sample(b, t - 1, k - 1)
                        for q in range(3):
                            if n in DCONV[q][0]:
                                width = DCONV[q][1]
                                first = width * DCONV[q][0].index(n)
                                dconv(b, q, nxt, range(first, first + width))
                        if nxt is not None:
                            front(nxt, n)
                dconv(b, 3, nxt, range(K))

            pe.nop().then_inc(s["turned"], TURNED0)
            pe.nop().then_inc(s["g_sample"], 1)
            pe.nop().then_inc(s["sampled"], SAMPLED0)
            pe.nop().then_inc(s["dconv_done"], DCONV0)
            pe.wait_ge(s["const_ready"], 3)
            pe.wait_ge(s["zeroed"], ZEROED)
            for step in range(2):
                first_mean(0, 1, step)
            for n in range(SLOTS):
                front(0, n)
                for step in range(2):
                    if n == REST[step]:
                        first_mean(1, B, step)
            with pe.Fori(0, B - 1) as b:
                batch_steps(b, b + 1)
            batch_steps(B - 1, None)
            with pe.If(is_beyond(pe)):
                general_path()

        @block.scalar
        def _(act):
            def first_std(lo, hi):
                act.wait_ge(s["first_var"], hi)
                act.activation(first_sd[:, lo:hi], psT[:, 0, B + lo:B + hi], ACT.Sqrt, bias=eps_col[:, :])\
                    .then_inc(s["first_sd"], hi - lo)

            def std(b):
                act.wait_ge(s["var_done"], b + 1)
                act.activation(sd[:, :], psB[:, 0, 1:2], ACT.Sqrt, bias=eps_col[:, :]).then_inc(s["sd_done"], 1)

            def front(b, n):
                if n == NORM1 + 2:
                    act.wait_ge(s["g_done"], b + 1)
                    act.activation(g_p[:, 0], g_sb[:, :], ACT.Copy).then_inc(s["g_hi_done"], 1)
                if n in SCORE:
                    i = SCORE.index(n)
                    for j in range(2):
                        act.wait_ge(s["simps_done"], 2 * (QT * b + i) + j + 1)
                        if i >= 1:
                            if j == (i - 1) // (QT // 2):
                                act.wait_ge(s["diagonal_done"], QT * b + i)
                            act.wait_ge(s["sim_done"], 2 * (QT * b + i - 1) + j + 1)
                        act.activation(rel[:, j, :], psB[:, j, :], ACT.Relu).then_inc(s["rel_done"], 1)
                if n == SPREAD2:
                    act.wait_ge(s["spread2_done"], b + 1)
                    act.activation(inv2_all[:, :], psB[:, :, :].rearrange("p j n -> p (j n)"), ACT.Copy)\
                        .then_inc(s["inv2_all_done"], 1)
                if n == VAR:
                    std(b)
                for which in range(2):
                    m = 2 * b + which
                    if 0 <= n - COMBINE[which] < V:
                        v = n - COMBINE[which]
                        act.wait_ge(s["combo_done"], V * m + v + 1)
                        act.activation(combo_p[:, 0, v], combo[:, v % 2], ACT.Copy).then_inc(s["combo_hi"], 1)
                    if n == CONV[which] + 3:
                        bias, width = ((b1_col, C), (b2_col, NOFF))[which]
                        act.wait_ge(s["m_done"], V * m + 2)
                        act.activation(m1[0:width], psA[0:width, 1, :], ACT.Identity, bias=bias[:, :])\
                            .then_inc(s["m1_done"], 1)

            def evacuate(b, t, what):
                n = TGROUPS * t + TURNS.index(what)
                kind, i = what.split()
                i = int(i)
                if what == TURNS[0]:
                    act.wait_ge(s["sampled"], len(VGROUPS) * (ROWT * b + t - 1) + SAMPLED0)
                act.wait_ge(s["turned"], TGROUPS * ROWT * b + n + 1 + TURNED0)
                if kind == "windows":
                    dst = hwin[:, t % 2, 4 * i:4 * i + 4, :].rearrange("q u c -> q (u c)")
                else:
                    dst = wcell[:, t % 2, i, :, :].rearrange("q g p -> q (g p)")
                act.activation(dst, psT[0:CELLS, n % 2, :], ACT.Copy).then_inc(s["turn_free"], 1)

            def relu_out(b, q):
                act.wait_ge(s["dconv_done"], 4 * b + q + 1 + DCONV0)
                bank = psB[:, DCONV_BANK[q], :]
                for t in range(2):
                    src = bank[:, t * P:(t + 1) * P].rearrange("p (u i j) -> p u i j", u=NBLK, i=BLK)
                    dst = orelu[:, q % 2, t * P:(t + 1) * P].rearrange("p (i u j) -> p u i j", u=NBLK, i=BLK)
                    last = act.activation(dst, src, ACT.Relu)
                last.then_inc(s["orelu_done"], 1)

            def general_path():
                with act.Fori(0, B) as b:
                    act.wait_ge(s["g_hT"], b + 1)
                    act.activation(scratch[:, :],
                                   psT[:, :, :].rearrange("p j n -> p (j n)"), ACT.Copy).then_inc(s["g_hTs"], 1)
                    act.wait_ge(s["g_hTs"], b + 1)
                    settle(act)
                    with act.Fori(0, ROWT) as t:
                        with act.Fori(0, QT) as m:
                            turn = K * (QT * (ROWT * b + t) + m)
                            act.wait_ge(s["g_sample"], turn + 1)
                            settle(act)
                            act.activation(h_cur, gxT[:, bass.ds(m, 1), :].rearrange("p i c -> p (i c)"), ACT.Copy)\
                                .then_inc(s["g_cur"], 1)
                            for k in range(K):
                                act.wait_ge(s["g_turn"], turn + k + 1)
                                act.activation(plane_t, psA[:, 0, :], ACT.Copy).then_inc(s["g_planeT"], 1)
                        act.wait_ge(s["g_conv"], ROWT * b + t + 1)
                        act.activation(orelu[:, 0, 0:P], psB[:, 1, 0:P], ACT.Relu).then_inc(s["g_relu"], 1)

            def batch_steps(b, nxt):
                for t in range(ROWT + 1):
                    for k in range(K):
                        n = K * t + k
                        if t < ROWT:
                            evacuate(b, t, f"tap {k}")
                            if k in WINDOWS_AT:
                                evacuate(b, t, f"windows {WINDOWS_AT[k]}")
                        for q in range(3):
                            if n == DCONV[q][0][-1]:
                                relu_out(b, q)
                        if nxt is not None:
                            front(nxt, n)
                relu_out(b, 3)

            act.nop().then_inc(s["turn_free"], 2)
            act.wait_ge(s["zeroed"], ZEROED)
            act.activation(table_col[:, :], eps_col[:, :], ACT.Sqrt)
            first_std(0, 1)
            for n in range(SLOTS):
                front(0, n)
                if n == REST[1]:
                    first_std(1, B)
                for i, w_p in enumerate(w_parts):
                    if n == W_HI[i]:
                        act.wait_ge(s["w_combined"], 2 * (i + 1))
                        for part_out, combined in zip(by_combo(w_p, 0), w_combos[i]):
                            act.activation(part_out, combined, ACT.Copy).then_inc(s["w_hi_done"], 1)
            with act.Fori(0, B - 1) as b:
                batch_steps(b, b + 1)
            batch_steps(B - 1, None)
            with act.If(is_beyond(act)):
                general_path()

        @block.vector
        def _(dve):
            def first_moments(lo, hi):
                for b in range(lo, hi):
                    for j in range(2):
                        dve.bn_stats(first_bn[:, b, j, :], x_all[:, b, j * HALF:(j + 1) * HALF])\
                            .then_inc(s["first_stats"], 1)
                for b in range(lo, hi):
                    dve.wait_ge(s["first_stats"], 2 * (b + 1))
                    dve.bn_aggr(first_mv[:, b, :], first_bn[:, b, :, :]).then_inc(s["first_moments"], 1)

            def first_spread(lo, hi):
                n = hi - lo
                dve.wait_ge(s["first_moments"], hi)
                dve.wait_ge(s["first_mean"], hi)
                dve.tensor_copy(first_norm[:, 0, lo:hi], psT[:, 0, lo:hi]).then_inc(s["first_dev"], n)
                dve.tensor_tensor(first_dev[:, lo:hi], first_mv[:, lo:hi, 0:1].rearrange("p b i -> p (b i)"),
                                  psT[:, 0, lo:hi], ALU.subtract).then_inc(s["first_dev"], n)
                dve.wait_ge(s["first_dev"], 3 * lo + 2 * n)
                dve.tensor_tensor(first_varp[:, lo:hi], first_dev[:, lo:hi], first_dev[:, lo:hi], ALU.mult)\
                    .then_inc(s["first_dev"], n)
                dve.wait_ge(s["first_dev"], 3 * hi)
                dve.tensor_tensor(first_varp[:, lo:hi], first_varp[:, lo:hi],
                                  first_mv[:, lo:hi, 1:2].rearrange("p b i -> p (b i)"), ALU.add)\
                    .then_inc(s["first_varp"], n)

            def first_rstd(lo, hi):
                dve.wait_ge(s["first_sd"], hi)
                dve.reciprocal(first_norm[:, 1, lo:hi], first_sd[:, lo:hi]).then_inc(s["first_done"], hi - lo)

            def channel_stats(b):
                settle(dve)
                for j in range(2):
                    dve.bn_stats(bn[:, j, :], batch(x_all, b)[:, j * HALF:(j + 1) * HALF])\
                        .then_inc(s["stats_done"], 1)
                dve.wait_ge(s["stats_done"], 2 * b + 2)
                settle(dve)
                dve.bn_aggr(mv[:, :], bn[:, :, :]).then_inc(s["moments"], 1)

            def spread(b):
                dve.wait_ge(s["moments"], b + 1)
                dve.wait_ge(s["mean_done"], b + 1)
                dve.tensor_copy(mean[:, :], psB[:, 0, 0:1]).then_inc(s["dev_done"], 1)
                dve.tensor_tensor(dev[:, :], mv[:, 0:1], psB[:, 0, 0:1], ALU.subtract).then_inc(s["dev_done"], 1)
                dve.wait_ge(s["dev_done"], 2 * b + 2)
                dve.scalar_tensor_tensor(out=varp[:, :], in0=dev[:, :], scalar=dev[:, :], in1=mv[:, 1:2],
                                         op0=ALU.mult, op1=ALU.add).then_inc(s["varp_done"], 1)

            def normalise_x(b):
                if isinstance(b, int):
                    dve.wait_ge(s["first_done"], b + 1)
                else:
                    dve.wait_ge(s["off_done"], 2 * b)
                for i, col in enumerate((mean, rstd)):
                    dve.tensor_copy(col[:, :], first_norm[:, i, bass.ds(b, 1)]).then_inc(s["first_picked"], 1)
                dve.wait_ge(s["first_picked"], 2 * b + 2)
                dve.tensor_scalar(g_sb[:, :], batch(x_all, b), mean[:, :], rstd[:, :], ALU.subtract, ALU.mult)\
                    .then_inc(s["g_done"], 1)

            def normalise_x1(b):
                dve.wait_ge(s["sd_done"], b + 1)
                dve.reciprocal(rstd[:, :], sd[:, :]).then_inc(s["rstd_done"], 1)
                dve.wait_ge(s["rstd_done"], b + 1)
                if isinstance(b, int):
                    dve.wait_ge(s["rims_zeroed"], RIMS)
                else:
                    dve.wait_ge(s["strips_bottom"], NBLK * b)
                dve.tensor_scalar(hpad[:, RIM:RIM + H, RIM:RIM + WID], batch(x_all, b).rearrange("p (h w) -> p h w", w=WID),
                                  mean[:, :], rstd[:, :], ALU.subtract, ALU.mult).then_inc(s["h_done"], 1)
                for i, col in enumerate((mean, rstd)):
                    dve.tensor_copy(norm2nd[:, bass.ds(b, 1), i:i + 1].rearrange("p b i -> p (b i)"), col[:, :])\
                        .then_inc(s["stat2_done"], 1)

            def inverse_norm2(b, i):
                m = QT * b + i + 1
                half = i // (QT // 2)
                dve.wait_ge(s["rel_done"], 2 * (m - 1) + half + 1)
                at = i % (QT // 2) * P
                dve.tensor_tensor(diagonal[:, :], rel[:, half, at:at + P], ident[:, :], ALU.mult)\
                    .then_inc(s["diagonal_done"], 1)
                dve.wait_ge(s["diagonal_done"], m)
                dve.tensor_reduce(norm2[:, i:i + 1], diagonal[:, :], AX.X, ALU.add).then_inc(s["norm2_done"], 1)
                dve.wait_ge(s["norm2_done"], m)
                dve.tensor_scalar(floor2[:, i:i + 1], norm2[:, i:i + 1], NORM_EPS ** 2, None, ALU.max)\
                    .then_inc(s["floor_done"], 1)
                dve.wait_ge(s["floor_done"], m)
                dve.reciprocal(inv2[:, i:i + 1], floor2[:, i:i + 1]).then_inc(s["inv2_done"], 1)

            def combine_weights(i):
                w, (_, plus, minus, _) = w_raw[i], w_combos[i]
                n = w.shape[1] // 3
                outer, middle, last = (w[:, r * n:(r + 1) * n] for r in range(3))
                if i == 0:
                    dve.wait_ge(s["conv_weights_in"], 5 * 16)
                dve.tensor_tensor(minus, outer, last, ALU.add).then_inc(s["w_half_sum"], 1)
                dve.wait_ge(s["w_half_sum"], 2 * i + 1)
                dve.tensor_scalar(minus, minus, 0.5, None, ALU.mult).then_inc(s["w_half_sum"], 1)
                dve.wait_ge(s["w_half_sum"], 2 * i + 2)
                for dst, sign in ((plus, 0.5), (minus, -0.5)):
                    dve.scalar_tensor_tensor(out=dst, in0=middle, scalar=sign, in1=minus, op0=ALU.mult, op1=ALU.add)\
                        .then_inc(s["w_combined"], 1)

            def split_weights(i):
                dve.wait_ge(s["w_hi_done"], V * (i + 1))
                for hi, lo, combined in zip(by_combo(w_parts[i], 0), by_combo(w_parts[i], 1), w_combos[i]):
                    dve.tensor_tensor(lo, combined, hi.bitcast(F32), ALU.subtract).then_inc(s["w_lo_done"], 1)

            def add_bias(b):
                dve.wait_ge(s["gx_done"], b + 1)
                dve.wait_ge(s["g_lo_done"], b + 1)
                dve.tensor_tensor(gxT_sum, psA[:, :, :].rearrange("p j (i c) -> p (j i) c", c=C),
                                  b0_row[:, :].unsqueeze(1).to_broadcast([P, QT, C]), ALU.add)\
                    .then_inc(s["gx_sum_done"], 1)

            def scale_gx(b, i):
                dve.wait_ge(s["gx_sum_done"], b + 1)
                dve.wait_ge(s["inv2_done"], QT * b + i + 1)
                dve.tensor_scalar(gxT[:, i, :], gxT_sum[:, i, :], inv2[:, i:i + 1], None, ALU.mult)\
                    .then_inc(s["gxT_done"], 1)

            def combine_rows(b, which, v):
                n = V * (2 * b + which) + v
                if which == 0 and v == 0:
                    dve.wait_ge(s["h_done"], b + 1)
                if which == 1 and v == 0:
                    dve.wait_ge(s["conv1_done"], 2 * b + 2)
                if not (isinstance(b, int) and n < 2):
                    dve.wait_ge(s["combo_lo"], n - 1)
                image = conv1_pad if which else hpad[:, RIM - 1:RIM + H + 1, RIM - 1:RIM + WID + 1]
                d0, d1 = (image[:, 0:H, :].rearrange("p (i e) c -> p i e c", e=2)[:, :, e, :] for e in range(2))
                d2, d3 = (image[:, 2:H + 2, :].rearrange("p (i e) c -> p i e c", e=2)[:, :, e, :] for e in range(2))
                a, op, c = ((d0, ALU.subtract, d2), (d1, ALU.add, d2), (d2, ALU.subtract, d1), (d1, ALU.subtract, d3))[v]
                dve.tensor_tensor(combo[:, v % 2], a, c, op).then_inc(s["combo_done"], 1)

            def split_rows(b, which, v):
                dve.wait_ge(s["combo_hi"], V * (2 * b + which) + v + 1)
                dve.tensor_tensor(combo_p[:, 1, v], combo[:, v % 2], combo_p[:, 0, v].bitcast(F32), ALU.subtract)\
                    .then_inc(s["combo_lo"], 1)

            def middle_sums(b, which):
                n, width = 2 * b + which, (C, NOFF)[which]
                dve.wait_ge(s["m1_done"], n + 1)
                dve.wait_ge(s["m_done"], V * n + 3)
                for dst, op in ((m1_plus, ALU.add), (m1_minus, ALU.subtract)):
                    dve.tensor_tensor(dst[0:width], m1[0:width], psB[0:width, 0, :], op).then_inc(s["m1_sums"], 1)

            def output_rows(b, which):
                n, width = 2 * b + which, (C, NOFF)[which]
                dve.wait_ge(s["m_done"], V * n + 4)
                dve.wait_ge(s["m1_sums"], 2 * n + 2)
                for e, (left, right, op) in enumerate(((m1_plus, psA[:, 0, :], ALU.add),
                                                       (m1_minus, psB[:, 1, :], ALU.subtract))):
                    if which:
                        dst = off_ch.rearrange("p (i e c) -> p i e c", e=2, c=WID)[:, :, e, :]
                    else:
                        dst = conv1_pad[:, 1:1 + H, 1:1 + WID].rearrange("p (i e) c -> p i e c", e=2)[:, :, e, :]
                    dve.tensor_tensor(dst, left[0:width].rearrange("p (i c) -> p i c", c=WID),
                                      right[0:width].rearrange("p (i c) -> p i c", c=WID), op)\
                        .then_inc(s["off_done" if which else "conv1_done"], 1)

            def add_mixed(b):
                dve.wait_ge(s["mix_done"], QT * (b + 1))
                dve.wait_ge(s["inv2_all_done"], b + 1)
                dve.tensor_tensor(scratch[:, :], psA[:, :, :].rearrange("p j n -> p (j n)"), inv2_all[:, :], ALU.mult)\
                    .then_inc(s["scaled_done"], 1)
                dve.wait_ge(s["scaled_done"], b + 1)
                xb = batch(x_all, b)
                dve.tensor_tensor(xb, xb, scratch[:, :], ALU.add).then_inc(s["x1_done"], 1)
                dve.wait_ge(s["x1_done"], b + 1)

            def front(b, n):
                if n == NORM1 + 2:
                    dve.wait_ge(s["g_hi_done"], b + 1)
                    dve.tensor_tensor(g_p[:, 1], g_sb[:, :], part(g_p, 0), ALU.subtract).then_inc(s["g_lo_done"], 1)
                if n in SCORE:
                    inverse_norm2(b, SCORE.index(n))
                if n == GX:
                    add_bias(b)
                if n in SCALE:
                    scale_gx(b, SCALE.index(n))
                if n == SCALE[-1]:
                    dve.tensor_tensor(inv2_diag[:, :, :], ident[:, :].unsqueeze(1).to_broadcast([P, QT, P]),
                                      inv2[:, :].unsqueeze(2).to_broadcast([P, QT, P]), ALU.mult)\
                        .then_inc(s["diag_done"], 1)
                if n == STATS:
                    add_mixed(b)
                    channel_stats(b)
                if n == MEAN:
                    spread(b)
                if n == NORM:
                    normalise_x1(b)
                for which in range(2):
                    if 0 <= n - COMBINE[which] < V:
                        combine_rows(b, which, n - COMBINE[which])
                    if 0 < n - COMBINE[which] <= V:
                        split_rows(b, which, n - COMBINE[which] - 1)
                    if n == CONV[which] + 4:
                        middle_sums(b, which)
                    if n == CONV[which] + 5:
                        output_rows(b, which)
                if n in TURN_OFF:
                    j = TURN_OFF.index(n)
                    dve.wait_ge(s["offT_done"], 2 * b + j + 1)
                    src = psA[:, j, 0:4 * NOFF].rearrange("p (n a) -> p n a", a=2)
                    dst = pos_all[:, bass.ds(b, 1), 4 * j:4 * j + 4, :].rearrange("p b t (n a) -> p (b t n) a", a=2)
                    dve.tensor_tensor(dst, src, grid[:, :].unsqueeze(1).to_broadcast([P, 4 * NOFF // 2, 2]),
                                      ALU.add).then_inc(s["pos_done"], 1)
                if n == EXTREMES:
                    dve.wait_ge(s["off_done"], 2 * b + 2)
                    for i, op in enumerate((ALU.max, ALU.min)):
                        dve.tensor_reduce(extremes[:, i, bass.ds(b, 1)], off_ch, AX.X, op)\
                            .then_inc(s["extremes_done"], 1)

            def tents(b, t):
                n = ROWT * b + t
                if t % (ROWT // 2) == 0:
                    dve.wait_ge(s["pos_done"], 2 * b + t // (ROWT // 2) + 1)
                if not (isinstance(b, int) and n == 0):
                    dve.wait_ge(s["weights_done"], K * n)
                p = pos_all[:, bass.ds(b, 1), t, :].rearrange("p b n -> p (b n)")
                dve.tensor_tensor(tent[:, :, :], p.unsqueeze(2).to_broadcast([P, NOFF, SUP]),
                                  cell_idx[:, :].unsqueeze(1).to_broadcast([P, NOFF, SUP]),
                                  ALU.subtract).then_inc(s["dist_done"], 1)
                dve.wait_ge(s["dist_done"], n + 1)
                dve.scalar_tensor_tensor(out=tent[:, :, :], in0=tent[:, :, :], scalar=-1.0, in1=tent[:, :, :],
                                         op0=ALU.mult, op1=ALU.min).then_inc(s["fold_done"], 1)
                dve.wait_ge(s["fold_done"], n + 1)
                dve.tensor_scalar(tent[:, :, :], tent[:, :, :], 1.0, 0.0, ALU.add, ALU.max)\
                    .then_inc(s["tent_done"], 1)

            def weights(b, t, k):
                if k == 0:
                    tents(b, t)
                    dve.wait_ge(s["tent_done"], ROWT * b + t + 1)
                if not (isinstance(b, int) and ROWT * b + t == 0):
                    dve.wait_ge(s["turned"], TGROUPS * (ROWT * b + t - 1) + TURNS.index(f"tap {k}") + 1 + TURNED0)
                ky, kx = divmod(k, 3)
                tv = tent[:, :, :].rearrange("p (g k a) r -> p g k a r", g=G, a=2)
                ty = tv[:, :, k, 0, :].unsqueeze(3).to_broadcast([P, G, SUP, SUP])
                tx = tv[:, :, k, 1, :].unsqueeze(2).to_broadcast([P, G, SUP, SUP])
                w = wpix[:, k, :, :].rearrange("p g (r c) -> p g r c", c=WIN)
                dve.tensor_tensor(w[:, :, ky:ky + SUP, kx:kx + SUP], ty, tx, ALU.mult)\
                    .then_inc(s["weights_done"], 1)

            def take_samples(b, t, v):
                n = len(VGROUPS) * t + v
                lo, hi = VGROUPS[v]
                dve.wait_ge(s["sampled"], len(VGROUPS) * ROWT * b + n + 1 + SAMPLED0)
                if v == 0 and t % 2 == 0:
                    dve.wait_ge(s["dconv_done"], 4 * b + t // 2 - 1 + DCONV0)
                dve.tensor_copy(val[:, t % 4, lo * K * BP:hi * K * BP], psV[:, n % 2, 0:(hi - lo) * K * BP])\
                    .then_inc(s["val_free"], 1)

            def add_out(b, q):
                dve.wait_ge(s["orelu_done"], 4 * b + q + 1)
                dve.wait_ge(out_sems[q % 2], 16 * (2 * b + q // 2 + 1))
                dve.tensor_tensor(yout[:, q % 2, :], orelu[:, q % 2, :],
                                  batch(x_all, b)[:, q * 2 * P:(q + 1) * 2 * P], ALU.add)\
                    .then_inc(s["yout_done"], 1)

            def find_farthest():
                dve.wait_ge(s["extremes_done"], 2 * B)
                dve.tensor_reduce(ends[:, 0:1], extremes[:, 0, :], AX.X, ALU.max).then_inc(s["ends_done"], 1)
                dve.tensor_reduce(ends[:, 1:2], extremes[:, 1, :], AX.X, ALU.min).then_inc(s["ends_done"], 1)
                dve.wait_ge(s["ends_done"], 2)
                dve.scalar_tensor_tensor(out=farthest[:, :], in0=ends[:, 1:2], scalar=-1.0, in1=ends[:, 0:1],
                                         op0=ALU.mult, op1=ALU.max).then_inc(s["farthest_done"], 1)
                dve.wait_ge(s["far_turned"], 1)
                dve.tensor_reduce(far_all[:, :], psA[0:1, 0, 0:NOFF], AX.X, ALU.max).then_inc(s["far_all_done"], 1)
                dve.wait_ge(s["far_all_done"], 1)
                dve.tensor_scalar(beyond[:, :], far_all[:, :], float(REACH), None, ALU.is_gt)\
                    .then_inc(s["flag_done"], 1)

            def general_tents(b, t):
                n = ROWT * b + t
                pos = pos_all[:, bass.ds(b, 1), bass.ds(t, 1), :].rearrange("p b t n -> p (b t n)")
                dve.tensor_tensor(place.rearrange("p (g k a) -> p g k a", g=G, a=2),
                                  pos.rearrange("p (g k a) -> p g k a", g=G, a=2),
                                  tap_at[:, :, :].unsqueeze(1).to_broadcast([P, G, K, 2]),
                                  ALU.add).then_inc(s["g_place"], 1)
                dve.tensor_copy(stat_cur[:, 2:3], row_at[:, bass.ds(t, 1)]).then_inc(s["g_place"], 1)
                dve.wait_ge(s["g_place"], 2 * n + 2)
                by_axis = place.rearrange("p (n a) -> p n a", a=2)
                rows = by_axis[:, :, 0:1].rearrange("p n o -> p (n o)")
                dve.tensor_scalar(rows, rows, stat_cur[:, 2:3], None, ALU.add).then_inc(s["g_shift"], 1)
                dve.wait_ge(s["g_shift"], n + 1)
                for a, dst in enumerate((tent_y, tent_x)):
                    m = 2 * n + a + 1
                    dve.tensor_tensor(wide_tmp, by_axis[:, :, a:a + 1].to_broadcast([P, GK, WID]),
                                      cell32[:, :].unsqueeze(1).to_broadcast([P, GK, WID]),
                                      ALU.subtract).then_inc(s["g_d1"], 1)
                    dve.wait_ge(s["g_d1"], m)
                    dve.scalar_tensor_tensor(out=dst, in0=wide_tmp, scalar=-1.0, in1=wide_tmp,
                                             op0=ALU.mult, op1=ALU.min).then_inc(s["g_f1"], 1)
                    dve.wait_ge(s["g_f1"], m)
                    dve.tensor_scalar(dst, dst, 1.0, 0.0, ALU.add, ALU.max).then_inc(s["g_tent"], 1)
                dve.memset(acc, 0.0).then_inc(s["g_zero"], 1)
                dve.wait_ge(s["g_tent"], 2 * n + 2)
                dve.wait_ge(s["g_zero"], n + 1)
                settle(dve)

            def general_path():
                dve.wait_ge(out_sems[0], 16 * (2 * B + 1))
                dve.wait_ge(s["stat2_done"], 2 * B)
                with dve.Fori(0, B) as b:
                    dve.tensor_copy(stat_cur[:, 0:2], norm2nd[:, bass.ds(b, 1), :].rearrange("p b i -> p (b i)"))\
                        .then_inc(s["g_stat"], 1)
                    dve.wait_ge(s["g_stat"], b + 1)
                    dve.tensor_scalar(g_sb[:, :], batch(x_all, b), stat_cur[:, 0:1], stat_cur[:, 1:2],
                                      ALU.subtract, ALU.mult).then_inc(s["g_h"], 1)
                    with dve.Fori(0, ROWT) as t:
                        general_tents(b, t)
                        with dve.Fori(0, QT) as m:
                            for k in range(K):
                                n = K * (QT * (ROWT * b + t) + m) + k
                                ty = tent_y.rearrange("p (g k) r -> p g k r", g=G)[:, :, k, bass.ds(BLK * m, BLK)]
                                tx = tent_x.rearrange("p (g k) c -> p g k c", g=G)[:, :, k, :]
                                dve.tensor_tensor(plane.rearrange("p (g r c) -> p g r c", g=G, r=BLK),
                                                  ty.unsqueeze(3).to_broadcast([P, G, BLK, WID]),
                                                  tx.unsqueeze(2).to_broadcast([P, G, BLK, WID]),
                                                  ALU.mult).then_inc(s["g_plane"], 1)
                                dve.wait_ge(s["g_sample"], n + 1 + 1)
                                dve.tensor_tensor(acc[:, k * P:(k + 1) * P], acc[:, k * P:(k + 1) * P], psV[:, 0, 0:P],
                                                  ALU.add)\
                                    .then_inc(s["g_acc"], 1)
                        n = ROWT * b + t
                        dve.wait_ge(s["g_relu"], n + 1)
                        dve.wait_ge(s["g_stored"], 16 * (n + 1))
                        dve.tensor_tensor(yout[:, 0, 0:P], orelu[:, 0, 0:P],
                                          batch(x_all, b)[:, bass.ds(P * t, P)], ALU.add)\
                            .then_inc(s["g_out"], 1)

            def batch_steps(b, nxt):
                if nxt is None:
                    find_farthest()
                for t in range(ROWT + 1):
                    for k in range(K):
                        n = K * t + k
                        if nxt is not None and n == NORM1:
                            normalise_x(nxt)
                        if t < ROWT - 1:
                            weights(b, t + 1, k)
                        if t >= 1 and k in SAMPLED_AT:
                            take_samples(b, t - 1, SAMPLED_AT.index(k))
                        for q in range(3):
                            if n == DCONV[q][0][-1] + 1:
                                add_out(b, q)
                        if nxt is not None:
                            front(nxt, n)
                if nxt is not None:
                    for k in range(K):
                        weights(nxt, 0, k)
                add_out(b, 3)

            dve.nop().then_inc(s["val_free"], 2)
            dve.wait_ge(s["zeroed"], ZEROED)
            dve.tensor_scalar(grid_i[:, 1:2], grid_i[:, 0:1], 5, None, ALU.arith_shift_right)\
                .then_inc(s["grid_ready"], 1)
            dve.tensor_scalar(grid_i[:, 2:3], grid_i[:, 0:1], BLK - 1, None, ALU.bitwise_and)\
                .then_inc(s["grid_ready"], 1)
            dve.wait_ge(s["grid_ready"], 2)
            dve.tensor_scalar(grid[:, :], grid_i[:, 1:3], float(REACH), None, ALU.add).then_inc(s["grid_ready"], 1)
            dve.wait_ge(s["grid_ready"], 3)
            dve.tensor_scalar(grid_i[:, 3:4], grid_i[:, 0:1], WID - BLK, None, ALU.bitwise_and)\
                .then_inc(s["grid_ready"], 1)
            dve.wait_ge(s["grid_ready"], 4)
            dve.tensor_copy(block_col[:, :], grid_i[:, 3:4]).then_inc(s["grid_ready"], 1)
            dve.wait_ge(s["grid_ready"], 5)
            dve.wait_ge(s["x_first_in"], 16)
            first_moments(0, 1)
            first_spread(0, 1)
            first_rstd(0, 1)
            normalise_x(0)
            for n in range(SLOTS):
                front(0, n)
                for b in range(1, B):
                    if n == SCALE[b]:
                        dve.wait_ge(s["x_rest_in"], 16)
                        first_moments(b, b + 1)
                if n == REST[0] + 2:
                    first_spread(1, B)
                if n == REST[1] + 2:
                    first_rstd(1, B)
                for i in range(len(w_parts)):
                    if n == W_COMBINE[i]:
                        combine_weights(i)
                    if n == W_LO[i]:
                        split_weights(i)
                if n == TURN_OFF[0]:
                    dve.wait_ge(s["rims_zeroed"], RIMS + 1)
                    for k in range(K):
                        weights(0, 0, k)
            dve.wait_ge(s["coords_ready"], 4)
            dve.tensor_scalar(tap_at[:, :, 1:2], tap_at[:, :, 1:2], block_col[:, :], None, ALU.add)\
                .then_inc(s["grid_ready"], 1)
            with dve.Fori(0, B - 1) as b:
                batch_steps(b, b + 1)
            batch_steps(B - 1, None)
            with dve.If(is_beyond(dve)):
                general_path()


def kernel(x, L0_conv_W, L0_conv_b, L1_conv_w1, L1_conv_b1, L1_conv_w2, L1_conv_b2, L1_conv_wd):
    import numpy as np
    import concourse.bacc as bacc
    from concourse.bass_utils import run_bass_kernel_spmd

    def taps_first(w):
        w = np.asarray(w)
        return np.ascontiguousarray(w.reshape(w.shape[0], w.shape[1], 9).transpose(1, 2, 0))

    arrays = {
        "x": np.ascontiguousarray(x),
        "W0": np.ascontiguousarray(np.asarray(L0_conv_W).T),
        "b0": np.ascontiguousarray(L0_conv_b),
        "w1": taps_first(L1_conv_w1),
        "b1": np.asarray(L1_conv_b1).reshape(-1, 1),
        "w2": taps_first(L1_conv_w2),
        "b2": np.asarray(L1_conv_b2).reshape(-1, 1),
        "wd": taps_first(L1_conv_wd),
    }
    nc = bacc.Bacc("TRN2", target_bir_lowering=False, num_devices=1)
    args = [nc.dram_tensor(n, a.shape, mybir.dt.from_np(a.dtype), kind="ExternalInput").ap()
            for n, a in arrays.items()]
    out = nc.dram_tensor("out", arrays["x"].shape, F32, kind="ExternalOutput").ap()
    mix_deform_kernel(nc, *args, out)
    r = run_bass_kernel_spmd(nc, [arrays], core_ids=[0])
    return r.results[0]["out"]
```
